# Optimizing a Trainium2 kernel written in Bass

```python
import numpy as np
import jax
import jax.numpy as jnp

def _softmax(x, axis=-1):
    return jax.nn.softmax(x, axis=axis)

def _gelu(x):
    return jax.nn.gelu(x, approximate=True)

def _silu(x):
    return jax.nn.silu(x)

def _sigmoid(x):
    return jax.nn.sigmoid(x)

def _layernorm(x, axis=-1, eps=1e-05):
    m = jnp.mean(x, axis=axis, keepdims=True)
    v = jnp.var(x, axis=axis, keepdims=True)
    return (x - m) / jnp.sqrt(v + eps)

def _scatter_add(tgt, idx, src, axis=0):
    return tgt.at[idx].add(src)

def _segment_sum(src, seg, n):
    return jax.ops.segment_sum(src, seg, n)
kernel_name = 'mk_perceiver_d1_seqx_r8_7749fd'

def setup_inputs(seed: int=0):
    np.random.seed(seed)
    _w = jnp.asarray

    def _rec_inputs():
        import jax
        import jax.numpy as jnp
        _rk = jax.random.key(seed)
        x = -0.0002928 + 1 * jax.random.normal(jax.random.fold_in(_rk, 1), (64, 32, 128), jnp.float32)
        _lenS = 32 - jax.random.randint(jax.random.fold_in(_rk, 7), (64,), 0, max(1, 32 // 4) + 1, jnp.int32)
        _lenS2 = 257 - jax.random.randint(jax.random.fold_in(_rk, 8), (64,), 0, max(1, 257 // 4) + 1, jnp.int32)
        _ctx_2048P = jax.random.normal(jax.random.fold_in(_rk, 11), (64, 16, 256), jnp.float32)
        _ctx_2048c = jax.random.dirichlet(jax.random.fold_in(_rk, 511), 0.3 * jnp.ones((16,), jnp.float32), (64, 257))
        _ctx_2048t = jnp.einsum('bsk,bkd->bsd', _ctx_2048c, _ctx_2048P)
        _ctx_2048t = _ctx_2048t * jax.lax.rsqrt(jnp.mean(jnp.square(_ctx_2048t)) + 1e-12) * 0.953939
        ctx_2048 = -0.000514642 + 1.00011 * (_ctx_2048t + 0.3 * jax.random.normal(jax.random.fold_in(_rk, 611), (64, 257, 256), jnp.float32))
        return (x, ctx_2048)
    x, ctx_2048 = _rec_inputs()

    def _L0_xattn_setup():
        import jax, jax.numpy as jnp
        import numpy as np
        NUM_HEADS = 16
        key = jax.random.key(seed)
        ks = jax.random.split(key, 5)
        dim = 128
        B, N, N_c = (4, 128, 32)
        x = jax.random.normal(ks[0], (B, N, dim), dtype=jnp.float32)
        context = jax.random.normal(ks[1], (B, N_c, 2 * dim), dtype=jnp.float32)
        w_qkv = jax.random.normal(ks[2], (3 * dim, dim), dtype=jnp.float32) * 0.02
        w_proj = jax.random.normal(ks[3], (dim, dim), dtype=jnp.float32) * 0.02
        b_proj = jax.random.normal(ks[4], (dim,), dtype=jnp.float32) * 0.02
        return {'x': x, 'context': context, 'w_qkv': w_qkv, 'w_proj': w_proj, 'b_proj': b_proj}
    _L0_xattn_all = _L0_xattn_setup()
    _L0_xattn_in = {k: v for k, v in _L0_xattn_all.items() if k in ('w_qkv', 'w_proj', 'b_proj')}
    del _L0_xattn_all

    def _L0_attn_setup():
        import jax, jax.numpy as jnp
        import numpy as np
        B, T, C, H = (2, 256, 128, 16)
        N = C // H
        TM_DIM, TD_DIM = (32, 64)
        EPS = 1e-05 * 8 ** 2

        def _forward(x, tmx, tmw, tmk, tmv, tmr, tmg, maa_w1, maa_w2, tdecay, td_w1, td_w2, u, Wr, Wk, Wv, Wg, Wo, ln_w, ln_b):
            Bq, Tq, Cq = x.shape
            xx = jnp.concatenate([jnp.zeros_like(x[:, :1]), x[:, :-1]], axis=1) - x
            xxx = x + xx * tmx
            t5 = jnp.tanh(xxx @ maa_w1).reshape(Bq, Tq, 5, TM_DIM)
            m = jnp.einsum('btfe,fec->fbtc', t5, maa_w2)
            xw = x + xx * (tmw + m[0])
            xk = x + xx * (tmk + m[1])
            xv = x + xx * (tmv + m[2])
            xr = x + xx * (tmr + m[3])
            xg = x + xx * (tmg + m[4])
            r = xr @ Wr
            k = xk @ Wk
            v = xv @ Wv
            g = jax.nn.silu(xg @ Wg)
            w = tdecay + jnp.tanh(xw @ td_w1) @ td_w2
            decay = jnp.exp(-jnp.exp(w))
            to_tbhn = lambda a: a.reshape(Bq, Tq, H, N).transpose(1, 0, 2, 3)
            rT, kT, vT, dT = (to_tbhn(a) for a in (r, k, v, decay))

            def step(S, inp):
                r_t, k_t, v_t, d_t = inp
                kv = k_t[..., :, None] * v_t[..., None, :]
                y = jnp.einsum('bhi,bhij->bhj', r_t, S + u[None, :, :, None] * kv)
                return (d_t[..., None] * S + kv, y)
            S0 = jnp.zeros((Bq, H, N, N), x.dtype)
            _, ys = jax.lax.scan(step, S0, (rT, kT, vT, dT))
            y = ys.transpose(1, 0, 2, 3).reshape(Bq, Tq, Cq)
            yh = y.reshape(Bq, Tq, H, N)
            mu = yh.mean(-1, keepdims=True)
            var = yh.var(-1, keepdims=True)
            yn = (yh - mu) / jnp.sqrt(var + EPS)
            yn = (yn * ln_w.reshape(H, N) + ln_b.reshape(H, N)).reshape(Bq, Tq, Cq)
            return yn * g @ Wo
        key = jax.random.key(seed)
        ks = jax.random.split(key, 16)
        nrm = lambda k, shp, s: jax.random.normal(k, shp, dtype=jnp.float32) * s
        uni = lambda k, shp, a: jax.random.uniform(k, shp, jnp.float32, -a, a)
        ddd = (jnp.arange(C, dtype=jnp.float32) / C).reshape(1, 1, C)
        return {'x': nrm(ks[0], (B, T, C), 1.0), 'time_maa_x': 1.0 - ddd ** 0.5, 'time_maa_w': 1.0 - ddd ** 0.5, 'time_maa_k': 1.0 - ddd ** 0.5, 'time_maa_v': 1.0 - (ddd ** 0.5 + 0.15), 'time_maa_r': 1.0 - ddd ** 0.25, 'time_maa_g': 1.0 - ddd ** 0.25, 'time_maa_w1': uni(ks[1], (C, 5 * TM_DIM), 0.0001), 'time_maa_w2': uni(ks[2], (5, TM_DIM, C), 0.0001), 'time_decay': jnp.linspace(-6.0, -1.0, C).astype(jnp.float32).reshape(1, 1, C), 'time_decay_w1': uni(ks[3], (C, TD_DIM), 0.0001), 'time_decay_w2': uni(ks[4], (TD_DIM, C), 0.0001), 'time_faaaa': nrm(ks[5], (H, N), 0.1), 'W_r': nrm(ks[6], (C, C), C ** (-0.5)), 'W_k': nrm(ks[7], (C, C), C ** (-0.5)), 'W_v': nrm(ks[8], (C, C), C ** (-0.5)), 'W_g': nrm(ks[9], (C, C), C ** (-0.5)), 'W_o': nrm(ks[10], (C, C), C ** (-0.5)), 'ln_w': jnp.ones((C,), jnp.float32), 'ln_b': jnp.zeros((C,), jnp.float32)}
    _L0_attn_all = _L0_attn_setup()
    _L0_attn_in = {k: v for k, v in _L0_attn_all.items() if k in ('time_maa_x', 'time_maa_w', 'time_maa_k', 'time_maa_v', 'time_maa_r', 'time_maa_g', 'time_maa_w1', 'time_maa_w2', 'time_decay', 'time_decay_w1', 'time_decay_w2', 'time_faaaa', 'W_r', 'W_k', 'W_v', 'W_g', 'W_o', 'ln_w', 'ln_b')}
    del _L0_attn_all

    def _L0_ffn_setup():
        import jax, jax.numpy as jnp
        import numpy as np
        B, S = (4, 64)
        H = 128
        I = 352
        E = 8
        K = 2
        IS = 176
        key = jax.random.key(seed)
        ks = jax.random.split(key, 8)

        def init(k, shape, fan_in):
            return (jax.random.normal(k, shape, jnp.float32) / np.sqrt(fan_in)).astype(jnp.float32)
        return {'hidden_states': jax.random.normal(ks[0], (B, S, H), jnp.float32), 'gate_w': init(ks[1], (H, E), H), 'Wg': init(ks[2], (E, H, I), H), 'Wu': init(ks[3], (E, H, I), H), 'Wd': init(ks[4], (E, I, H), I), 'Sg': init(ks[5], (H, IS), H), 'Su': init(ks[6], (H, IS), H), 'Sd': init(ks[7], (IS, H), IS)}
    _L0_ffn_all = _L0_ffn_setup()
    _L0_ffn_in = {k: v for k, v in _L0_ffn_all.items() if k in ('gate_w', 'Wg', 'Wu', 'Wd', 'Sg', 'Su', 'Sd')}
    del _L0_ffn_all
    return {'x': x, 'ctx_2048': ctx_2048, 'L0_xattn_w_qkv': _L0_xattn_in['w_qkv'], 'L0_xattn_w_proj': _L0_xattn_in['w_proj'], 'L0_xattn_b_proj': _L0_xattn_in['b_proj'], 'L0_attn_time_maa_x': _L0_attn_in['time_maa_x'], 'L0_attn_time_maa_w': _L0_attn_in['time_maa_w'], 'L0_attn_time_maa_k': _L0_attn_in['time_maa_k'], 'L0_attn_time_maa_v': _L0_attn_in['time_maa_v'], 'L0_attn_time_maa_r': _L0_attn_in['time_maa_r'], 'L0_attn_time_maa_g': _L0_attn_in['time_maa_g'], 'L0_attn_time_maa_w1': _L0_attn_in['time_maa_w1'], 'L0_attn_time_maa_w2': _L0_attn_in['time_maa_w2'], 'L0_attn_time_decay': _L0_attn_in['time_decay'], 'L0_attn_time_decay_w1': _L0_attn_in['time_decay_w1'], 'L0_attn_time_decay_w2': _L0_attn_in['time_decay_w2'], 'L0_attn_time_faaaa': _L0_attn_in['time_faaaa'], 'L0_attn_W_r': _L0_attn_in['W_r'], 'L0_attn_W_k': _L0_attn_in['W_k'], 'L0_attn_W_v': _L0_attn_in['W_v'], 'L0_attn_W_g': _L0_attn_in['W_g'], 'L0_attn_W_o': _L0_attn_in['W_o'], 'L0_attn_ln_w': _L0_attn_in['ln_w'], 'L0_attn_ln_b': _L0_attn_in['ln_b'], 'L0_ffn_gate_w': _L0_ffn_in['gate_w'], 'L0_ffn_Wg': _L0_ffn_in['Wg'], 'L0_ffn_Wu': _L0_ffn_in['Wu'], 'L0_ffn_Wd': _L0_ffn_in['Wd'], 'L0_ffn_Sg': _L0_ffn_in['Sg'], 'L0_ffn_Su': _L0_ffn_in['Su'], 'L0_ffn_Sd': _L0_ffn_in['Sd']}

def reference(x, ctx_2048, L0_xattn_w_qkv, L0_xattn_w_proj, L0_xattn_b_proj, L0_attn_time_maa_x, L0_attn_time_maa_w, L0_attn_time_maa_k, L0_attn_time_maa_v, L0_attn_time_maa_r, L0_attn_time_maa_g, L0_attn_time_maa_w1, L0_attn_time_maa_w2, L0_attn_time_decay, L0_attn_time_decay_w1, L0_attn_time_decay_w2, L0_attn_time_faaaa, L0_attn_W_r, L0_attn_W_k, L0_attn_W_v, L0_attn_W_g, L0_attn_W_o, L0_attn_ln_w, L0_attn_ln_b, L0_ffn_gate_w, L0_ffn_Wg, L0_ffn_Wu, L0_ffn_Wd, L0_ffn_Sg, L0_ffn_Su, L0_ffn_Sd):
    import jax
    import jax.numpy as jnp

    def _L0_xattn_ref(x, context, w_qkv, w_proj, b_proj):
        import jax, jax.numpy as jnp
        import numpy as np
        NUM_HEADS = 16
        B, N, C = x.shape
        H = NUM_HEADS
        D = C // H
        scale = D ** (-0.5)
        qkv = (x @ w_qkv.T).reshape(B, N, 3, H, D).transpose(2, 0, 3, 1, 4)
        q, k, v = (qkv[0], qkv[1], qkv[2])
        N_c = context.shape[1]
        kv = context.reshape(B, N_c, 2, H, D).transpose(2, 0, 3, 1, 4)
        extra_k, extra_v = (kv[0], kv[1])
        k = jnp.concatenate([extra_k, k], axis=2)
        v = jnp.concatenate([extra_v, v], axis=2)
        dtype = q.dtype
        attn = jnp.einsum('bhnd,bhmd->bhnm', q * scale, k).astype(jnp.float32)
        attn = jax.nn.softmax(attn, axis=-1).astype(dtype)
        out = jnp.einsum('bhnm,bhmd->bhnd', attn, v)
        out = out.transpose(0, 2, 1, 3).reshape(B, N, C)
        return out @ w_proj.T + b_proj

    def _L0_attn_ref(x, time_maa_x, time_maa_w, time_maa_k, time_maa_v, time_maa_r, time_maa_g, time_maa_w1, time_maa_w2, time_decay, time_decay_w1, time_decay_w2, time_faaaa, W_r, W_k, W_v, W_g, W_o, ln_w, ln_b):
        import jax, jax.numpy as jnp
        import numpy as np
        B, T, C, H = (2, 256, 128, 16)
        N = C // H
        TM_DIM, TD_DIM = (32, 64)
        EPS = 1e-05 * 8 ** 2

        def _forward(x, tmx, tmw, tmk, tmv, tmr, tmg, maa_w1, maa_w2, tdecay, td_w1, td_w2, u, Wr, Wk, Wv, Wg, Wo, ln_w, ln_b):
            Bq, Tq, Cq = x.shape
            xx = jnp.concatenate([jnp.zeros_like(x[:, :1]), x[:, :-1]], axis=1) - x
            xxx = x + xx * tmx
            t5 = jnp.tanh(xxx @ maa_w1).reshape(Bq, Tq, 5, TM_DIM)
            m = jnp.einsum('btfe,fec->fbtc', t5, maa_w2)
            xw = x + xx * (tmw + m[0])
            xk = x + xx * (tmk + m[1])
            xv = x + xx * (tmv + m[2])
            xr = x + xx * (tmr + m[3])
            xg = x + xx * (tmg + m[4])
            r = xr @ Wr
            k = xk @ Wk
            v = xv @ Wv
            g = jax.nn.silu(xg @ Wg)
            w = tdecay + jnp.tanh(xw @ td_w1) @ td_w2
            decay = jnp.exp(-jnp.exp(w))
            to_tbhn = lambda a: a.reshape(Bq, Tq, H, N).transpose(1, 0, 2, 3)
            rT, kT, vT, dT = (to_tbhn(a) for a in (r, k, v, decay))

            def step(S, inp):
                r_t, k_t, v_t, d_t = inp
                kv = k_t[..., :, None] * v_t[..., None, :]
                y = jnp.einsum('bhi,bhij->bhj', r_t, S + u[None, :, :, None] * kv)
                return (d_t[..., None] * S + kv, y)
            S0 = jnp.zeros((Bq, H, N, N), x.dtype)
            _, ys = jax.lax.scan(step, S0, (rT, kT, vT, dT))
            y = ys.transpose(1, 0, 2, 3).reshape(Bq, Tq, Cq)
            yh = y.reshape(Bq, Tq, H, N)
            mu = yh.mean(-1, keepdims=True)
            var = yh.var(-1, keepdims=True)
            yn = (yh - mu) / jnp.sqrt(var + EPS)
            yn = (yn * ln_w.reshape(H, N) + ln_b.reshape(H, N)).reshape(Bq, Tq, Cq)
            return yn * g @ Wo
        return _forward(x, time_maa_x, time_maa_w, time_maa_k, time_maa_v, time_maa_r, time_maa_g, time_maa_w1, time_maa_w2, time_decay, time_decay_w1, time_decay_w2, time_faaaa, W_r, W_k, W_v, W_g, W_o, ln_w, ln_b)

    def _L0_ffn_ref(hidden_states, gate_w, Wg, Wu, Wd, Sg, Su, Sd):
        import jax, jax.numpy as jnp
        import numpy as np
        B, S = (4, 64)
        H = 128
        I = 352
        E = 8
        K = 2
        IS = 176
        b, s, h = hidden_states.shape
        x = hidden_states.reshape(-1, h)
        T = x.shape[0]
        logits = x @ gate_w
        top_v, top_i = jax.lax.top_k(logits, K)
        top_p = jax.nn.softmax(top_v, axis=-1)
        combine = jnp.zeros((T, E), x.dtype).at[jnp.arange(T)[:, None], top_i].add(top_p)
        g = jnp.einsum('th,ehi->tei', x, Wg)
        u = jnp.einsum('th,ehi->tei', x, Wu)
        d = jnp.einsum('tei,eih->teh', jax.nn.silu(g) * u, Wd)
        expert_out = jnp.einsum('te,teh->th', combine, d)
        shared = jax.nn.silu(x @ Sg) * (x @ Su) @ Sd
        return (expert_out + shared).reshape(b, s, h)
    x = x + _L0_xattn_ref(_layernorm(x, axis=-1), ctx_2048, L0_xattn_w_qkv, L0_xattn_w_proj, L0_xattn_b_proj)
    x = x + _L0_attn_ref(_layernorm(x, axis=-1), L0_attn_time_maa_x, L0_attn_time_maa_w, L0_attn_time_maa_k, L0_attn_time_maa_v, L0_attn_time_maa_r, L0_attn_time_maa_g, L0_attn_time_maa_w1, L0_attn_time_maa_w2, L0_attn_time_decay, L0_attn_time_decay_w1, L0_attn_time_decay_w2, L0_attn_time_faaaa, L0_attn_W_r, L0_attn_W_k, L0_attn_W_v, L0_attn_W_g, L0_attn_W_o, L0_attn_ln_w, L0_attn_ln_b)
    x = x + _L0_ffn_ref(_layernorm(x, axis=-1), L0_ffn_gate_w, L0_ffn_Wg, L0_ffn_Wu, L0_ffn_Wd, L0_ffn_Sg, L0_ffn_Su, L0_ffn_Sd)
    return x

_drawn_inputs = setup_inputs


def setup_inputs(seed=0):
    import zlib

    import numpy as np

    out = dict(_drawn_inputs(seed))
    spreads = {'L0_attn_ln_w': (1.0, 0.2), 'L0_attn_ln_b': (0.0, 0.1)}
    factors = {'L0_attn_time_maa_x': 64.0,
     'L0_attn_time_maa_w': 64.0,
     'L0_attn_time_maa_w1': 64.0,
     'L0_attn_time_maa_w2': 64.0,
     'L0_attn_time_decay_w1': 64.0,
     'L0_attn_time_decay_w2': 64.0}
    for name, (base, spread) in spreads.items():
        noise = np.random.default_rng([zlib.crc32(name.encode()), seed]).standard_normal(out[name].shape)
        drawn = base * np.exp(spread * noise) if base else spread * noise
        out[name] = jnp.asarray(drawn.astype(out[name].dtype))
    for name, factor in factors.items():
        out[name] = (out[name] * factor).astype(out[name].dtype)
    return out
```

```python
from contextlib import ExitStack

import concourse.bass as bass
from concourse import mybir

F32 = mybir.dt.float32
ALU = mybir.AluOpType
ACT = mybir.ActivationFunctionType
AX = mybir.AxisListType

P = 128
C = 128
B = 64
N = 32
NT = B * N // P
BLK = 512
NB = B * N // BLK
TPB = BLK // P
SPB = BLK // N
H = 16
D = C // H
G = 4
HG = H // G
NCTX = 257
KC = 2
KEYS = NCTX + N
LN_EPS = 1e-5
GN_EPS = 1e-5 * 64
TM = 32
TD = 64
E = 8
I = 352
IS = 176
PAR_X, PAR_W, PAR_K, PAR_V, PAR_R, PAR_G, PAR_DECAY, PAR_BONUS, PAR_LN_W, PAR_LN_B = range(10)
NPAR = 10
W_R, W_K, W_V, W_G, W_O = range(5)


TIME_W_DMAS = 20
FFN_W_DMAS = 10


def expert_chunks(width):
    n = -(-width // P)
    size = -(-width // (16 * n)) * 16
    return [(s, min(size, width - s)) for s in range(0, width, size)]


def perceiver_layer(nc, t, out):
    x_tiles = t["x"].rearrange("b n c -> (b n) c").rearrange("(t p) c -> p t c", p=P)
    out_tiles = out.rearrange("b n c -> (b n) c").rearrange("(t p) c -> p t c", p=P)
    ctx_dram = t["ctx_2048"]

    with ExitStack() as whole:
        def sem(name):
            return whole.enter_context(nc.semaphore(name))

        def sb(name, shape, scope=whole):
            return scope.enter_context(nc.sbuf_tensor(name, shape, F32))

        psum = whole.enter_context(nc.psum_tensor("psum", [P, 8, BLK], F32))
        bank = [psum[:, i, :] for i in range(8)]

        x_res = sb("x_res", [P, NT, C])
        x_cen = sb("x_cen", [P, NT, C])
        x_sq = sb("x_sq", [P, NT, C])
        ln_T = sb("ln_T", [P, B * N])
        ln_sum = sb("ln_sum", [P, NT])
        ln_negmean = sb("ln_negmean", [P, NT])
        ln_sqsum = sb("ln_sqsum", [P, NT])
        ln_var = sb("ln_var", [P, NT])
        ln_rstd = sb("ln_rstd", [P, NT])
        minus_half = sb("minus_half", [P, NT])
        ones = sb("ones", [P, G])
        ident = sb("ident", [P, P])
        head_of = sb("head_of", [P, H])
        quad_of = sb("quad_of", [P, G])
        same_head = sb("same_head", [P, P])
        same_head_mean = sb("same_head_mean", [P, P])

        mix_w1 = sb("mix_w1", [P, 5 * TM])
        mix_w2 = sb("mix_w2", [P, C])
        mix_w2_last = sb("mix_w2_last", [TM, C])
        decay_w1 = sb("decay_w1", [P, TD])
        decay_w2 = sb("decay_w2", [TD, C])
        w_time = sb("w_time", [P, 5, C])
        param_rows = sb("param_rows", [NPAR, C])
        gate_w = sb("gate_w", [P, E])
        w_gate = sb("w_gate", [P, E, I])
        w_up = sb("w_up", [P, E, I])
        w_down = sb("w_down", [P, E, len(expert_chunks(I)), C])
        ws_gate = sb("ws_gate", [P, IS])
        ws_up = sb("ws_up", [P, IS])
        ws_down = sb("ws_down", [P, len(expert_chunks(IS)), C])

        s_time_w_in = sem("s_time_w_in")
        s_ffn_w_in = sem("s_ffn_w_in")
        s_x_in = [sem(f"s_x_in{i}") for i in range(NB)]
        s_ln_sum = sem("s_ln_sum")
        s_ln_negmean = sem("s_ln_negmean")
        s_ln_cen = sem("s_ln_cen")
        s_ln_sq = sem("s_ln_sq")
        s_ln_sqsum = sem("s_ln_sqsum")
        s_ln_var = sem("s_ln_var")
        s_ln_rstd = sem("s_ln_rstd")
        s_ln_norm = sem("s_ln_norm")
        s_ln_turned = sem("s_ln_turned")
        s_ln_T = sem("s_ln_T")
        s_const = sem("s_const")

        def ln_vector(v, which, x_ready=None):
            at = NB * which
            for n in range(NB):
                tiles = slice(TPB * n, TPB * n + TPB)
                if x_ready:
                    x_ready(n)
                nc.vector.tensor_reduce(ln_sum[:, tiles], x_res[:, tiles, :], AX.X, ALU.add).then_inc(s_ln_sum, 1)
                v.wait_ge(s_ln_sum, at + n + 1)
                nc.vector.tensor_scalar(ln_negmean[:, tiles], ln_sum[:, tiles], -1.0 / C, None, ALU.mult).then_inc(s_ln_negmean, 1)
                v.wait_ge(s_ln_negmean, at + n + 1)
                nc.vector.tensor_tensor(x_cen[:, tiles, :], x_res[:, tiles, :],
                                        ln_negmean[:, tiles].unsqueeze(2).broadcast_to([P, TPB, C]),
                                        ALU.add).then_inc(s_ln_cen, 1)
            for n in range(NB):
                tiles = slice(TPB * n, TPB * n + TPB)
                v.wait_ge(s_ln_sq, at + n + 1)
                nc.vector.tensor_reduce(ln_sqsum[:, tiles], x_sq[:, tiles, :], AX.X, ALU.add).then_inc(s_ln_sqsum, 1)
                v.wait_ge(s_ln_sqsum, at + n + 1)
                nc.vector.tensor_scalar(ln_var[:, tiles], ln_sqsum[:, tiles], 1.0 / C, LN_EPS,
                                        ALU.mult, ALU.add).then_inc(s_ln_var, 1)
            for n in range(NB):
                tiles = slice(TPB * n, TPB * n + TPB)
                v.wait_ge(s_ln_rstd, at + n + 1)
                nc.vector.tensor_tensor(x_cen[:, tiles, :], x_cen[:, tiles, :],
                                        ln_rstd[:, tiles].unsqueeze(2).broadcast_to([P, TPB, C]),
                                        ALU.mult).then_inc(s_ln_norm, 1)

        def ln_scalar_square(act, which):
            for n in range(NB):
                tiles = slice(TPB * n, TPB * n + TPB)
                act.wait_ge(s_ln_cen, NB * which + n + 1)
                nc.scalar.activation(x_sq[:, tiles, :], x_cen[:, tiles, :], ACT.Square).then_inc(s_ln_sq, 1)

        def ln_scalar_evacuate(act, which, banks):
            for n in range(NB):
                act.wait_ge(s_ln_turned, NB * which + n + 1)
                nc.scalar.copy(ln_T[:, BLK * n:BLK * n + BLK], bank[banks[n % 2]][:]).then_inc(s_ln_T, 1)

        def ln_gpsimd(pool, which):
            for n in range(NB):
                tiles = slice(TPB * n, TPB * n + TPB)
                pool.wait_ge(s_ln_var, NB * which + n + 1)
                nc.gpsimd.tensor_tensor(ln_rstd[:, tiles], ln_var[:, tiles], minus_half[:, tiles],
                                        ALU.pow).then_inc(s_ln_rstd, 1)

        def ln_tensor(pe, which, banks):
            for n in range(NB):
                pe.wait_ge(s_ln_norm, NB * which + n + 1)
                if n >= 2:
                    pe.wait_ge(s_ln_T, NB * which + n - 1)
                for k in range(TPB):
                    last = pe.transpose(bank[banks[n % 2]][:, P * k:P * k + P], x_cen[:, TPB * n + k, :], ident[:])
                last.then_inc(s_ln_turned, 1)

        with ExitStack() as scope:
            NSLOT = 4
            w_rows = sb("w_rows", [P, 4, C], scope)
            w_T = sb("w_T", [P, 4, C], scope)
            b_rows = sb("b_rows", [P, C], scope)
            qT = sb("qT", [P, B * N], scope)
            k_own = sb("k_own", [P, B, N + 1], scope)
            v_tok = sb("v_tok", [P, NT, C], scope)
            v_quad = sb("v_quad", [P, B, C], scope)
            k_left = sb("k_left", [B, C], scope)
            attn_T = sb("attn_T", [P, B * N], scope)
            kv_in = sb("kv_in", [P, NSLOT, KC, 2 * C], scope)
            v_left_in = sb("v_left_in", [G, NSLOT, C], scope)
            q_heads = sb("q_heads", [P, 2, H, N], scope)
            kT = sb("kT", [P, 2, KEYS], scope)
            probs = sb("probs", [P, 2, G, KEYS], scope)
            probs_own = sb("probs_own", [P, 2, G, N], scope)
            probs_left = sb("probs_left", [P, 2, G], scope)
            neg_max = sb("neg_max", [P, 2, G], scope)
            row_sum = sb("row_sum", [P, 2, G], scope)
            inv_sum = sb("inv_sum", [P, 2, G], scope)
            pT = sb("pT", [P, 2, 2, BLK], scope)
            pT_own = sb("pT_own", [P, 2, P], scope)
            pT_left = sb("pT_left", [G, 2, P], scope)
            v_own_diag = sb("v_own_diag", [P, 2, C], scope)
            v_left_diag = sb("v_left_diag", [G, 2, C], scope)
            inv_spread = sb("inv_spread", [P, 2, C], scope)
            o_masked = sb("o_masked", [P, HG, N], scope)
            o_sum = sb("o_sum", [P, N], scope)
            head_in_group = sb("head_in_group", [P, HG], scope)
            head_scaled = sb("head_scaled", [P, H], scope)
            query_of = sb("query_of", [P, N], scope)

            s_w_in = sem("s_w_in")
            s_kleft_in = sem("s_kleft_in")
            s_masks = sem("s_masks")
            s_masks_dve = sem("s_masks_dve")
            s_w_turned = sem("s_w_turned")
            s_w_T = sem("s_w_T")
            s_proj = sem("s_proj")
            s_qT = sem("s_qT")
            s_k_own = sem("s_k_own")
            s_v_tok = sem("s_v_tok")
            s_v_quad = [sem(f"s_v_quad{i}") for i in range(NB)]
            s_ctx_in = [sem(f"s_ctx_in{i}") for i in range(NSLOT)]
            s_ready_q = sem("s_ready_q")
            s_ready_v = sem("s_ready_v")
            s_spread = sem("s_spread")
            s_scores = sem("s_scores")
            s_max = sem("s_max")
            s_exp = sem("s_exp")
            s_probs_own = sem("s_probs_own")
            s_pT = sem("s_pT")
            s_pT_out = sem("s_pT_out")
            s_keys = sem("s_keys")
            s_keys_out = sem("s_keys_out")
            s_inv = sem("s_inv")
            s_pv = sem("s_pv")
            s_o_masked = sem("s_o_masked")
            s_o_sum = sem("s_o_sum")
            s_attn = sem("s_attn")
            s_proj_out = sem("s_proj_out")
            s_proj_bias = sem("s_proj_bias")
            s_x1 = sem("s_x1")

            S_BANK = [(0, 1), (2, 3)]
            PT_BANK = [4, 5]
            KEY_BANK = bank[6]
            O_BANK = bank[7]
            own = slice(NCTX - 1, NCTX - 1 + N)

            def over_sequences(eng, step):
                for u in range(NSLOT):
                    step(u, u)
                with eng.Fori(1, B // NSLOT - 1) as turn:
                    for u in range(NSLOT):
                        step(turn * NSLOT + u, u)
                for u in range(NSLOT):
                    step(B - NSLOT + u, u)

            def loaded(b, u):
                return b * (32 // NSLOT) + (32 - u * (32 // NSLOT))

            def queries_of(b):
                return bass.ds(b * N, N)

            def first(b, n):
                return isinstance(b, int) and b < n

            block = scope.enter_context(nc.Block())

            @block.sync
            def _(sp):
                for n in range(NB):
                    sp.dma_start(x_res[:, TPB * n:TPB * n + TPB, :], x_tiles[:, TPB * n:TPB * n + TPB, :]).then_inc(s_x_in[n], 16)
                sp.dma_start(w_rows[:, 0:3, :], t["L0_xattn_w_qkv"].rearrange("(s o) c -> o s c", s=3)).then_inc(s_w_in, 16)
                sp.dma_start(w_rows[:, 3, :], t["L0_xattn_w_proj"]).then_inc(s_w_in, 16)
                sp.dma_start(b_rows[:], t["L0_xattn_b_proj"].rearrange("(a c) -> a c", a=1).broadcast_to([P, C])).then_inc(s_w_in, 16)
                sp.dma_start(k_left[:], ctx_dram[:, NCTX - 1, 0:C]).then_inc(s_kleft_in, 16)

                def load(b, u):
                    if not first(b, NSLOT):
                        sp.wait_ge(s_pv, b - NSLOT + 1)
                        sp.wait_ge(s_ready_v, b - NSLOT + 1)
                    sp.dma_start(kv_in[:, u, :, :], ctx_dram[bass.ds(b, 1), 0:NCTX - 1, :].rearrange(
                        "a (p c) d -> p (a c) d", c=KC)).then_inc(s_ctx_in[u], 16)
                    sp.dma_start(v_left_in[:, u, :], ctx_dram[bass.ds(b, 1), NCTX - 1, C:2 * C].broadcast_to([G, C])
                                 ).then_inc(s_ctx_in[u], 16)

                for u in range(NSLOT):
                    load(u, u)
                sp.dma_start(mix_w1[:], t["L0_attn_time_maa_w1"]).then_inc(s_time_w_in, 16)
                mix_w2_rows = t["L0_attn_time_maa_w2"].rearrange("f e c -> (f e) c")
                sp.dma_start(mix_w2[:], mix_w2_rows[0:4 * TM, :]).then_inc(s_time_w_in, 16)
                sp.dma_start(mix_w2_last[:], mix_w2_rows[4 * TM:5 * TM, :]).then_inc(s_time_w_in, 16)
                sp.dma_start(decay_w1[:], t["L0_attn_time_decay_w1"]).then_inc(s_time_w_in, 16)
                sp.dma_start(decay_w2[:], t["L0_attn_time_decay_w2"]).then_inc(s_time_w_in, 16)
                for k, name in enumerate(["W_r", "W_k", "W_v", "W_g", "W_o"]):
                    sp.dma_start(w_time[:, k, :], t["L0_attn_" + name]).then_inc(s_time_w_in, 16)
                for k, name in enumerate(["time_maa_x", "time_maa_w", "time_maa_k", "time_maa_v", "time_maa_r",
                                          "time_maa_g", "time_decay"]):
                    sp.dma_start(param_rows[k:k + 1, :], t["L0_attn_" + name].rearrange("a b c -> (a b) c")).then_inc(s_time_w_in, 16)
                sp.dma_start(param_rows[PAR_BONUS:PAR_BONUS + 1, :],
                             t["L0_attn_time_faaaa"].rearrange("(a h) d -> a (h d)", a=1)).then_inc(s_time_w_in, 16)
                for k, name in ((PAR_LN_W, "ln_w"), (PAR_LN_B, "ln_b")):
                    sp.dma_start(param_rows[k:k + 1, :], t["L0_attn_" + name].rearrange("(a c) -> a c", a=1)).then_inc(s_time_w_in, 16)
                sp.dma_start(gate_w[:], t["L0_ffn_gate_w"]).then_inc(s_ffn_w_in, 16)
                sp.dma_start(w_gate[:], t["L0_ffn_Wg"].rearrange("e h i -> h e i")).then_inc(s_ffn_w_in, 16)
                sp.dma_start(w_up[:], t["L0_ffn_Wu"].rearrange("e h i -> h e i")).then_inc(s_ffn_w_in, 16)
                for k, (start, size) in enumerate(expert_chunks(I)):
                    sp.dma_start(w_down[0:size, :, k, :],
                                 t["L0_ffn_Wd"][:, start:start + size, :].rearrange("e i c -> i e c")).then_inc(s_ffn_w_in, 16)
                sp.dma_start(ws_gate[:], t["L0_ffn_Sg"]).then_inc(s_ffn_w_in, 16)
                sp.dma_start(ws_up[:], t["L0_ffn_Su"]).then_inc(s_ffn_w_in, 16)
                for k, (start, size) in enumerate(expert_chunks(IS)):
                    sp.dma_start(ws_down[0:size, k, :], t["L0_ffn_Sd"][start:start + size, :]).then_inc(s_ffn_w_in, 16)
                for n in range(NB):
                    sp.wait_ge(s_v_tok, n + 1)
                    for q in range(TPB):
                        for g in range(G):
                            sp.dma_start(
                                v_quad[N * g:N * g + N, SPB * n:SPB * n + SPB, :].rearrange("p (t q) c -> p t q c", q=TPB)[:, :, q, :],
                                v_tok[N * q:N * q + N, TPB * n:TPB * n + TPB, :]).then_inc(s_v_quad[n], 16)
                with sp.Fori(1, B // NSLOT) as turn:
                    for u in range(NSLOT):
                        load(turn * NSLOT + u, u)

            @block.gpsimd
            def _(pool):
                g = nc.gpsimd
                made = [0]

                def link(ins):
                    made[0] += 1
                    ins.then_inc(s_const, 1)
                    pool.wait_ge(s_const, made[0])

                g.memset(minus_half[:], -0.5)
                g.memset(ones[:], 1.0)
                g.memset(head_of[:], 1.0)
                g.memset(quad_of[:], 1.0)
                link(g.memset(ident[:], 0.0))
                g.affine_select(out=ident[:], in_=ident[:], compare_op=ALU.not_equal, fill=1.0, base=0,
                                pattern=[[-1, P]], channel_multiplier=1)
                g.affine_select(out=head_of[:], in_=head_of[:], compare_op=ALU.is_ge, fill=0.0, base=0,
                                pattern=[[-D, H]], channel_multiplier=1)
                link(g.affine_select(out=quad_of[:], in_=quad_of[:], compare_op=ALU.is_ge, fill=0.0, base=0,
                                     pattern=[[-N, G]], channel_multiplier=1))
                g.affine_select(out=head_of[:], in_=head_of[:], compare_op=ALU.is_ge, fill=0.0, base=D - 1,
                                pattern=[[D, H]], channel_multiplier=-1)
                g.affine_select(out=quad_of[:], in_=quad_of[:], compare_op=ALU.is_ge, fill=0.0, base=N - 1,
                                pattern=[[N, G]], channel_multiplier=-1).then_inc(s_masks, 1)
                pool.wait_ge(s_masks, 1)
                g.tensor_copy(same_head[:].rearrange("p (h d) -> p h d", h=H),
                              head_of[:].unsqueeze(2).broadcast_to([P, H, D])).then_inc(s_masks, 1)
                ln_gpsimd(pool, 0)
                pool.wait_ge(s_masks_dve, 2)

                def ready_q(b, par):
                    n = b // SPB if isinstance(b, int) else None
                    if first(b, B):
                        pool.wait_ge(s_qT, n + 1)
                        pool.wait_ge(s_k_own, n + 2)
                    if not first(b, 2):
                        pool.wait_ge(s_scores, 2 * b - 2)
                    g.tensor_tensor(q_heads[:, par], qT[:, queries_of(b)].unsqueeze(1).broadcast_to([P, H, N]),
                                    head_scaled[:].unsqueeze(2).broadcast_to([P, H, N]), ALU.mult)
                    g.tensor_copy(kT[:, par, NCTX - 1:KEYS], k_own[:, bass.ds(b, 1), :].rearrange("p a n -> p (a n)")).then_inc(s_ready_q, 1)

                def ready_v(b, u, par):
                    if isinstance(b, int):
                        pool.wait_ge(s_v_quad[b // SPB], 16 * TPB * G)
                    pool.wait_ge(s_ctx_in[u], loaded(b, u))
                    if not first(b, 2):
                        pool.wait_ge(s_pv, b - 1)
                    g.tensor_tensor(v_own_diag[:, par].rearrange("p (g c) -> p g c", g=G),
                                    v_quad[:, bass.ds(b, 1), :].rearrange("p a (g c) -> p (a g) c", g=G),
                                    quad_of[:].unsqueeze(2).broadcast_to([P, G, C // G]), ALU.mult)
                    g.tensor_tensor(v_left_diag[:, par].rearrange("p (g c) -> p g c", g=G),
                                    v_left_in[:, u, :].rearrange("p (g c) -> p g c", g=G),
                                    ident[0:G, 0:G].unsqueeze(2).broadcast_to([G, G, C // G]), ALU.mult).then_inc(s_ready_v, 1)

                def spread(b, par):
                    pool.wait_ge(s_inv, b + 1)
                    if not first(b, 2):
                        pool.wait_ge(s_pv, b - 1)
                    g.tensor_tensor(inv_spread[:, par].rearrange("p (g h d) -> p g h d", g=G, h=HG),
                                    quad_of[:].unsqueeze(1).unsqueeze(3).broadcast_to([P, G, HG, D]),
                                    inv_sum[:, par].unsqueeze(2).unsqueeze(3).broadcast_to([P, G, HG, D]),
                                    ALU.mult).then_inc(s_spread, 1)

                def pack_own(b, par):
                    pool.wait_ge(s_exp, 2 * b + 2)
                    if not first(b, 2):
                        pool.wait_ge(s_keys, b + 1)
                    g.tensor_tensor(probs_own[:, par], probs[:, par, :, own],
                                    ones[:].unsqueeze(2).broadcast_to([P, G, N]), ALU.mult)
                    g.tensor_copy(probs_left[:, par], probs[:, par, :, KEYS - 1]).then_inc(s_probs_own, 1)

                ready_q(0, 0)

                def step(b, u):
                    if not first(b, 1):
                        pack_own(b - 1, (u + 1) % 2)
                    if not (isinstance(b, int) and b == B - 1):
                        ready_q(b + 1, (u + 1) % 2)
                    ready_v(b, u, u % 2)
                    if not first(b, 1):
                        spread(b - 1, (u + 1) % 2)

                for u in range(NSLOT):
                    step(u, u)
                pool.wait_ge(s_qT, NB)
                pool.wait_ge(s_k_own, NB + 1)
                for n in range(NB):
                    pool.wait_ge(s_v_quad[n], 16 * TPB * G)
                with pool.Fori(1, B // NSLOT - 1) as turn:
                    for u in range(NSLOT):
                        step(turn * NSLOT + u, u)
                for u in range(NSLOT):
                    step(B - NSLOT + u, u)
                pack_own(B - 1, 1)
                spread(B - 1, 1)

            @block.scalar
            def _(act):
                ln_scalar_square(act, 0)
                act.wait_ge(s_w_turned, 1)
                nc.scalar.copy(w_T[:].rearrange("p s o -> p (s o)"), bank[6][:]).then_inc(s_w_T, 1)
                act.wait_ge(s_w_turned, 2)
                nc.scalar.copy(k_own[:, :, N], bank[7][:, 0:B]).then_inc(s_k_own, 1)
                ln_scalar_evacuate(act, 0, (0, 1))
                for n in range(NB):
                    act.wait_ge(s_proj, 3 * n + 1)
                    nc.scalar.copy(qT[:, BLK * n:BLK * n + BLK], bank[2][:]).then_inc(s_qT, 1)
                    act.wait_ge(s_proj, 3 * n + 2)
                    nc.scalar.copy(k_own[:, SPB * n:SPB * n + SPB, 0:N],
                                   bank[3][:].rearrange("p (b n) -> p b n", n=N)).then_inc(s_k_own, 1)
                    act.wait_ge(s_proj, 3 * n + 3)
                    nc.scalar.copy(v_tok[:, TPB * n:TPB * n + TPB, :].rearrange("p t c -> p (t c)"),
                                   bank[4][:]).then_inc(s_v_tok, 1)

                def keys_out(b, par_keys, par_probs, lag, lead):
                    act.wait_ge(s_keys, b + 2)
                    if lag:
                        nc.scalar.copy(pT_own[:, par_probs], KEY_BANK[:, 256:384])
                        last = nc.scalar.copy(pT_left[:, par_probs], KEY_BANK[0:G, 384:512])
                    if lead:
                        last = nc.scalar.copy(kT[:, par_keys, 0:NCTX - 1], KEY_BANK[:, 0:256])
                    last.then_inc(s_keys_out, 1)

                keys_out(-1, 0, 0, False, True)

                def step(b, u):
                    par = u % 2
                    for h in range(2):
                        if h == 1:
                            keys_out(b, (u + 1) % 2, (u + 1) % 2, not first(b, 1),
                                     not (isinstance(b, int) and b == B - 1))
                        act.wait_ge(s_max, 2 * b + (h + 1))
                        if h == 0 and not first(b, 2):
                            act.wait_ge(s_pT, 2 * b - 2)
                            act.wait_ge(s_probs_own, b - 1)
                            act.wait_ge(s_inv, b - 1)
                        for k in range(2):
                            gr = 2 * h + k
                            last = nc.scalar.activation(probs[:, par, gr, :], bank[S_BANK[h][k]][:, 0:KEYS], ACT.Exp,
                                                        bias=neg_max[:, par, gr:gr + 1],
                                                        accum_out=row_sum[:, par, gr:gr + 1])
                        last.then_inc(s_exp, 1)

                over_sequences(act, step)
                keys_out(B, 0, 1, True, False)

            @block.tensor
            def _(pe):
                pe.wait_ge(s_w_in, 48)
                pe.wait_ge(s_masks, 1)
                for k in range(4):
                    last = pe.transpose(bank[6][:, P * k:P * k + P], w_rows[:, k, :], ident[:])
                last.then_inc(s_w_turned, 1)
                pe.wait_ge(s_kleft_in, 16)
                pe.transpose(bank[7][:, 0:B], k_left[:], ident[0:B, 0:B]).then_inc(s_w_turned, 1)
                ln_tensor(pe, 0, (0, 1))
                pe.wait_ge(s_w_T, 1)
                for n in range(NB):
                    pe.wait_ge(s_ln_T, n + 1)
                    cols = slice(BLK * n, BLK * n + BLK)
                    if n:
                        pe.wait_ge(s_qT, n)
                    pe.matmul(bank[2][:], w_T[:, 0, :], ln_T[:, cols], start=True, stop=True).then_inc(s_proj, 1)
                    if n:
                        pe.wait_ge(s_k_own, n + 1)
                    pe.matmul(bank[3][:], w_T[:, 1, :], ln_T[:, cols], start=True, stop=True).then_inc(s_proj, 1)
                    if n:
                        pe.wait_ge(s_v_tok, n)
                    for k in range(TPB):
                        last = pe.matmul(bank[4][:, C * k:C * k + C], ln_T[:, BLK * n + P * k:BLK * n + P * k + P],
                                         w_T[:, 2, :], start=True, stop=True)
                    last.then_inc(s_proj, 1)

                def keys(b, u, par_probs, lag, lead):
                    if lead:
                        pe.wait_ge(s_ctx_in[u], loaded(b + 1, u))
                        for c in range(KC):
                            last = pe.transpose(KEY_BANK[:, P * c:P * c + P], kv_in[:, u, c, 0:C], ident[:])
                    if lag:
                        pe.wait_ge(s_probs_own, b)
                        pe.transpose(KEY_BANK[:, 256:384], probs_own[:, par_probs].rearrange("p g n -> p (g n)"), ident[:])
                        last = pe.transpose(KEY_BANK[0:G, 384:512], probs_left[:, par_probs], ident[:])
                    last.then_inc(s_keys, 1)

                def turn_probs(b, par, h):
                    pe.wait_ge(s_exp, 2 * b + (h + 1))
                    if not first(b, 1):
                        pe.wait_ge(s_pT_out, 2 * b + (h - 1))
                    for k in range(2):
                        for c in range(KC):
                            last = pe.transpose(bank[PT_BANK[h]][:, P * (2 * k + c):P * (2 * k + c) + P],
                                                probs[:, par, 2 * h + k, P * c:P * c + P], ident[:])
                    last.then_inc(s_pT, 1)

                def values(b, u, par):
                    pe.wait_ge(s_pT_out, 2 * b + 2)
                    if not first(b, 1):
                        pe.wait_ge(s_attn, b)
                    for c in range(KC):
                        for gr in range(G):
                            rows = slice(N * gr, N * gr + N)
                            pe.matmul(O_BANK[rows, 0:P], kv_in[:, u, c, C + N * gr:C + N * gr + N],
                                      pT[:, par, gr // 2, P * (2 * (gr % 2) + c):P * (2 * (gr % 2) + c) + P],
                                      start=(c == 0), stop=False, skip_group_check=True)
                    pe.wait_ge(s_ready_v, b + 1)
                    pe.wait_ge(s_keys_out, b + 3)
                    pe.matmul(O_BANK[:, 0:P], v_own_diag[:, par], pT_own[:, par], start=False, stop=False, skip_group_check=True)
                    pe.matmul(O_BANK[:, 0:P], v_left_diag[:, par], pT_left[:, par], start=False, stop=True, skip_group_check=True)
                    pe.wait_ge(s_spread, b + 1)
                    pe.matmul(O_BANK[:, P:P + N], inv_spread[:, par], query_of[:], start=True, stop=True,
                              skip_group_check=True).then_inc(s_pv, 1)

                keys(-1, 0, 0, False, True)
                pe.wait_ge(s_masks_dve, 2)

                def step(b, u):
                    par, before = u % 2, (u + 1) % 2
                    for h in range(2):
                        if h == 0:
                            pe.wait_ge(s_ready_q, b + 1)
                            pe.wait_ge(s_keys_out, b + 1)
                        if not first(b, 1):
                            pe.wait_ge(s_exp, 2 * b + (h - 1))
                        elif h == 0:
                            pe.wait_ge(s_k_own, NB + 1)
                            pe.wait_ge(s_v_tok, NB)
                            pe.wait_ge(s_ln_T, NB)
                        for k in range(2):
                            gr = 2 * h + k
                            last = pe.matmul(bank[S_BANK[h][k]][:, 0:KEYS],
                                             q_heads[:, par, HG * gr:HG * gr + HG, :].rearrange("p h n -> p (h n)"),
                                             kT[:, par, :], start=True, stop=True)
                        last.then_inc(s_scores, 1)
                        if h == 0:
                            if not first(b, 1):
                                turn_probs(b - 1, before, 1)
                            keys(b, (u + 1) % NSLOT, before, not first(b, 1),
                                 not (isinstance(b, int) and b == B - 1))
                        else:
                            turn_probs(b, par, 0)
                            if not first(b, 1):
                                values(b - 1, (u - 1) % NSLOT, before)

                over_sequences(pe, step)
                turn_probs(B - 1, 1, 1)
                pe.wait_ge(s_keys_out, B + 1)
                keys(B, 0, 1, True, False)
                values(B - 1, NSLOT - 1, 1)

                for n in range(NB):
                    pe.wait_ge(s_attn, B)
                    if n >= 2:
                        pe.wait_ge(s_proj_bias, n - 1)
                    for k in range(TPB):
                        last = pe.matmul(bank[n % 2][:, C * k:C * k + C], attn_T[:, BLK * n + P * k:BLK * n + P * k + P],
                                         w_T[:, 3, :], start=True, stop=True)
                    last.then_inc(s_proj_out, 1)

            @block.vector
            def _(v):
                v.wait_ge(s_masks, 1)
                nc.vector.tensor_reduce(head_in_group[:], head_of[:].rearrange("p (g h) -> p h g", g=G), AX.X,
                                        ALU.add).then_inc(s_masks_dve, 1)
                nc.vector.tensor_reduce(query_of[:], ident[:].rearrange("p (q n) -> p n q", n=N), AX.X, ALU.add)
                nc.vector.tensor_scalar(head_scaled[:], head_of[:], float(D) ** -0.5, None,
                                        ALU.mult).then_inc(s_masks_dve, 1)
                v.wait_ge(s_masks, 2)
                nc.vector.tensor_scalar(same_head_mean[:], same_head[:], 1.0 / D, None, ALU.mult).then_inc(s_masks_dve, 1)
                ln_vector(v, 0, lambda n: v.wait_ge(s_x_in[n], 16))

                def probs_out(b, par, h):
                    v.wait_ge(s_pT, 2 * b + (h + 1))
                    if not first(b, 2) and h == 0:
                        v.wait_ge(s_pv, b - 1)
                    nc.vector.tensor_copy(pT[:, par, h, :], bank[PT_BANK[h]][:]).then_inc(s_pT_out, 1)

                def normalise(b):
                    v.wait_ge(s_pv, b + 1)
                    nc.vector.tensor_tensor(o_masked[:], O_BANK[:, 0:P].rearrange("p (h n) -> p h n", h=HG),
                                            head_in_group[:].unsqueeze(2).broadcast_to([P, HG, N]),
                                            ALU.mult).then_inc(s_o_masked, 1)
                    v.wait_ge(s_o_masked, b + 1)
                    nc.vector.tensor_reduce(o_sum[:], o_masked[:].rearrange("p h n -> p n h"), AX.X, ALU.add).then_inc(s_o_sum, 1)
                    v.wait_ge(s_o_sum, b + 1)
                    nc.vector.tensor_tensor(attn_T[:, queries_of(b)], o_sum[:], O_BANK[:, P:P + N], ALU.mult).then_inc(s_attn, 1)

                def step(b, u):
                    par, before = u % 2, (u + 1) % 2
                    for h in range(2):
                        v.wait_ge(s_scores, 2 * b + (h + 1))
                        if h == 0 and not first(b, 2):
                            v.wait_ge(s_exp, 2 * b - 2)
                        nc.vector.tensor_reduce(
                            neg_max[:, par, 2 * h:2 * h + 2], psum[:, 2 * h:2 * h + 2, 0:KEYS], AX.X, ALU.max, negate=True).then_inc(s_max, 1)
                        if h == 0:
                            if not first(b, 2):
                                normalise(b - 2)
                            if not first(b, 1):
                                probs_out(b - 1, before, 1)
                        else:
                            if not first(b, 1):
                                inverse(b - 1, before)
                            probs_out(b, par, 0)

                def inverse(b, par):
                    v.wait_ge(s_exp, 2 * b + 2)
                    if not first(b, 2):
                        v.wait_ge(s_spread, b - 1)
                    nc.vector.reciprocal(inv_sum[:, par], row_sum[:, par]).then_inc(s_inv, 1)

                over_sequences(v, step)
                normalise(B - 2)
                probs_out(B - 1, 1, 1)
                inverse(B - 1, 1)
                normalise(B - 1)
                for n in range(NB):
                    v.wait_ge(s_proj_out, n + 1)
                    tiles = slice(TPB * n, TPB * n + TPB)
                    nc.vector.tensor_tensor(x_sq[:, tiles, :], bank[n % 2][:].rearrange("p (t c) -> p t c", c=C),
                                            b_rows[:].unsqueeze(1).broadcast_to([P, TPB, C]), ALU.add).then_inc(s_proj_bias, 1)
                    v.wait_ge(s_proj_bias, n + 1)
                    nc.vector.tensor_tensor(x_res[:, tiles, :], x_res[:, tiles, :], x_sq[:, tiles, :], ALU.add).then_inc(s_x1, 1)


        with ExitStack() as scope:
            def tile(name, shape):
                return sb(name, shape, scope)

            params = tile("params", [P, NPAR])
            v_weight = tile("v_weight", [P, D, C])
            to_column = tile("to_column", [P, D, C])
            diff = tile("diff", [P, 2, BLK])
            mixed_x = tile("mixed_x", [P, BLK])
            mix_hidden = tile("mix_hidden", [P, BLK])
            mix_hidden_last = tile("mix_hidden_last", [TM, BLK])
            mix_part = tile("mix_part", [P, 2, BLK])
            mixed = tile("mixed", [P, 2, 5, BLK])
            decay_hidden = tile("decay_hidden", [TD, BLK])
            decay_exp = tile("decay_exp", [P, BLK])
            decay = tile("decay", [P, 2, BLK])
            recep = tile("recep", [P, 2, BLK])
            key = tile("key", [P, 2, BLK])
            value = tile("value", [P, BLK])
            gate = tile("gate", [P, 2, BLK])
            bonus_in = tile("bonus_in", [P, BLK])
            bonus = tile("bonus", [P, 2, BLK])
            kv = tile("kv", [P, 2, BLK])
            state = tile("state", [P, 2, BLK])
            read = tile("read", [P, 2, BLK])
            y_sum = tile("y_sum", [P, BLK])
            y_cen = tile("y_cen", [P, BLK])
            y_sq = tile("y_sq", [P, BLK])
            y_var = tile("y_var", [P, BLK])
            y_invvar = tile("y_invvar", [P, BLK])
            y_rstd = tile("y_rstd", [P, BLK])
            y_norm = tile("y_norm", [P, BLK])
            y_affine = tile("y_affine", [P, BLK])
            y_gated = tile("y_gated", [P, BLK])

            names = """s_params_turned s_params s_vweight s_tocolumn s_diff s_mixed_x s_hidden s_hidden_out
                s_mix s_mix_out s_mixed s_dproj s_dhidden s_dproj2 s_dexp s_decay s_decay_cut
                s_recep s_key s_value s_gate s_bonus_in s_bonus s_kv s_state s_read s_y s_y_sum
                s_mean s_y_cen s_y_sq s_var s_y_var s_y_invvar s_y_rstd s_y_norm s_y_affine s_y_gated s_out
                s_x2 s_used s_read_zero""".split()
            (s_params_turned, s_params, s_vweight, s_tocolumn, s_diff, s_mixed_x, s_hidden, s_hidden_out,
             s_mix, s_mix_out, s_mixed, s_dproj, s_dhidden, s_dproj2, s_dexp, s_decay, s_decay_cut,
             s_recep, s_key, s_value, s_gate, s_bonus_in, s_bonus, s_kv, s_state, s_read, s_y, s_y_sum,
             s_mean, s_y_cen, s_y_sq, s_var, s_y_var, s_y_invvar, s_y_rstd, s_y_norm, s_y_affine, s_y_gated, s_out,
             s_x2, s_used, s_read_zero) = [sem(n) for n in names]
            s_prod = sem("s_prod")
            s_prod_free = [sem("s_prod_free0"), sem("s_prod_free1")]

            HIDDEN, HIDDEN_LAST, MIX = bank[0], bank[1], (2, 3)
            PROD, Y, POST = (4, 5), bank[6], bank[7]
            SEQ, WITHIN = "p (s n) -> p s n", N

            order = [("mix", 0)]
            for n in range(NB):
                order.append(("project", n))
                if n + 1 < NB:
                    order.append(("mix", n + 1))
                for j in range(D):
                    order.append(("state", n, j))
                    if n and j in (0, 2, 6):
                        order.append((("mean", "variance", "output")[(0, 2, 6).index(j)], n - 1))
                order.append(("sum", n))
            order += [("mean", NB - 1), ("variance", NB - 1), ("output", NB - 1)]
            prod_no = {}
            for s in order:
                if s[0] == "project":
                    for k in ("decay1", "decay2", "r", "k", "v", "g", "bonus"):
                        prod_no[(k, s[1])] = len(prod_no)
                elif s[0] == "state":
                    prod_no[("state", s[1], s[2])] = len(prod_no)

            def prod_bank(key_):
                return bank[PROD[prod_no[key_] % 2]]

            block = scope.enter_context(nc.Block())

            @block.gpsimd
            def _(pool):
                g = nc.gpsimd
                ln_gpsimd(pool, 1)
                g.memset(read[:], 0.0)
                g.memset(to_column[:], 0.0).then_inc(s_read_zero, 1)
                pool.wait_ge(s_time_w_in, 16 * TIME_W_DMAS)
                for j in range(D):
                    last = g.tensor_copy(v_weight[:, j, :].rearrange("p (h i) -> p h i", h=H),
                                         w_time[:, W_V, :].rearrange("p (h j) -> p h j", h=H)[:, :, j:j + 1].broadcast_to([P, H, D]))
                last.then_inc(s_vweight, 1)
                pool.wait_ge(s_read_zero, 1)
                for j in range(D):
                    last = g.tensor_copy(to_column[:, j, :].rearrange("p (h j) -> p h j", h=H)[:, :, j], head_of[:])
                last.then_inc(s_tocolumn, 1)
                for s in order:
                    n = s[1]
                    par = n % 2
                    if s[0] == "mix":
                        for f in range(5):
                            pool.wait_ge(s_mix_out, 5 * n + f + 1)
                            if n >= 2:
                                pool.wait_ge(s_prod, prod_no[("g", n - 2)] + 1)
                            g.tensor_tensor(mixed[:, par, f, :], mix_part[:, (5 * n + f) % 2, :],
                                            ln_T[:, BLK * n:BLK * n + BLK], ALU.add).then_inc(s_mixed, 1)
                    elif s[0] == "project":
                        pool.wait_ge(s_decay, n + 1)
                        g.memset(decay[:, par].rearrange(SEQ, n=N)[:, :, 0:1], 0.0).then_inc(s_decay_cut, 1)
                    elif s[0] == "state":
                        j = s[2]
                        q = D * n + j
                        pool.wait_ge(s_state, q + 1)
                        pool.wait_ge(s_recep, n + 1)
                        if q >= 2:
                            pool.wait_ge(s_y, q - 1)
                        g.tensor_tensor(read[:, q % 2].rearrange(SEQ, n=N)[:, :, 1:N],
                                        recep[:, par].rearrange(SEQ, n=N)[:, :, 1:N],
                                        state[:, q % 2].rearrange(SEQ, n=N)[:, :, 0:N - 1], ALU.mult).then_inc(s_read, 1)
                    elif s[0] == "output":
                        pool.wait_ge(s_y_rstd, n + 1)
                        if n:
                            pool.wait_ge(s_y_affine, n)
                        g.tensor_tensor(y_norm[:], y_cen[:], y_rstd[:], ALU.mult).then_inc(s_y_norm, 1)
                        pool.wait_ge(s_y_affine, n + 1)
                        if n:
                            pool.wait_ge(s_out, n)
                        g.tensor_tensor(y_gated[:], y_affine[:], gate[:, par], ALU.mult).then_inc(s_y_gated, 1)

            @block.scalar
            def _(act):
                ln_scalar_square(act, 1)
                ln_scalar_evacuate(act, 1, (0, 1))
                act.wait_ge(s_params_turned, 1)
                nc.scalar.copy(params[:], bank[2][:, 0:NPAR]).then_inc(s_params, 1)

                for s in order:
                    n = s[1]
                    par = n % 2
                    if s[0] == "mix":
                        act.wait_ge(s_hidden, n + 1)
                        if n:
                            act.wait_ge(s_mix, 5 * n)
                        nc.scalar.activation(mix_hidden[:], HIDDEN[:], ACT.Tanh)
                        nc.scalar.activation(mix_hidden_last[:], HIDDEN_LAST[0:TM, :], ACT.Tanh).then_inc(s_hidden_out, 1)
                    elif s[0] == "project":
                        act.wait_ge(s_params, 1)
                        act.wait_ge(s_prod, prod_no[("decay1", n)] + 1)
                        nc.scalar.activation(decay_hidden[:], prod_bank(("decay1", n))[0:TD, :], ACT.Tanh).then_inc(s_dhidden, 1)
                        act.wait_ge(s_prod, prod_no[("decay2", n)] + 1)
                        nc.scalar.activation(decay_exp[:], prod_bank(("decay2", n)), ACT.Exp,
                                             bias=params[:, PAR_DECAY:PAR_DECAY + 1]).then_inc(s_dexp, 1)
                        act.wait_ge(s_dexp, n + 1)
                        if n >= 2:
                            act.wait_ge(s_state, D * (n - 1))
                        nc.scalar.activation(decay[:, par], decay_exp[:], ACT.Exp, scale=-1.0).then_inc(s_decay, 1)
                        act.wait_ge(s_prod, prod_no[("r", n)] + 1)
                        if n >= 2:
                            act.wait_ge(s_read, D * (n - 1))
                        nc.scalar.copy(recep[:, par], prod_bank(("r", n))).then_inc(s_recep, 1)
                        act.wait_ge(s_prod, prod_no[("k", n)] + 1)
                        if n >= 2:
                            act.wait_ge(s_kv, D * (n - 1))
                        nc.scalar.copy(key[:, par], prod_bank(("k", n))).then_inc(s_key, 1)
                        act.wait_ge(s_prod, prod_no[("v", n)] + 1)
                        if n:
                            act.wait_ge(s_bonus, n)
                        nc.scalar.copy(value[:], prod_bank(("v", n))).then_inc(s_value, 1)
                        act.wait_ge(s_prod, prod_no[("g", n)] + 1)
                        if n >= 2:
                            act.wait_ge(s_y_gated, n - 1)
                        nc.scalar.activation(gate[:, par], prod_bank(("g", n)), ACT.Silu).then_inc(s_gate, 1)
                    elif s[0] == "variance":
                        act.wait_ge(s_y_cen, n + 1)
                        if n:
                            act.wait_ge(s_var, n)
                        nc.scalar.activation(y_sq[:], y_cen[:], ACT.Square).then_inc(s_y_sq, 1)
                    elif s[0] == "output":
                        act.wait_ge(s_y_invvar, n + 1)
                        if n:
                            act.wait_ge(s_y_norm, n)
                        nc.scalar.activation(y_rstd[:], y_invvar[:], ACT.Sqrt).then_inc(s_y_rstd, 1)

            @block.tensor
            def _(pe):
                pe.wait_ge(s_time_w_in, 16 * TIME_W_DMAS)
                pe.transpose(bank[2][:, 0:NPAR], param_rows[:], ident[0:NPAR, 0:NPAR]).then_inc(s_params_turned, 1)
                ln_tensor(pe, 1, (0, 1))

                def freed_by(key_):
                    n = key_[1]
                    return {"decay1": (s_dhidden, n + 1), "decay2": (s_dexp, n + 1), "r": (s_recep, n + 1),
                            "k": (s_key, n + 1), "v": (s_value, n + 1), "g": (s_gate, n + 1),
                            "bonus": (s_bonus, n + 1), "state": (s_kv, D * n + key_[-1] + 1)}[key_[0]]

                by_no = {no: key_ for key_, no in prod_no.items()}

                def product(key_, lhsT, rhs, rows=P):
                    no = prod_no[key_]
                    if no >= 2:
                        pe.wait_ge(*freed_by(by_no[no - 2]))
                    pe.matmul(prod_bank(key_)[0:rows, :], lhsT, rhs, start=True, stop=True).then_inc(s_prod, 1)

                for s in order:
                    n = s[1]
                    par = n % 2
                    if s[0] == "mix":
                        pe.wait_ge(s_mixed_x, n + 1)
                        if n == 0:
                            pe.wait_ge(s_ln_T, 2 * NB)
                        else:
                            pe.wait_ge(s_hidden_out, n)
                        pe.matmul(HIDDEN, mix_w1[:, 0:4 * TM], mixed_x[:], start=True, stop=True)
                        pe.matmul(HIDDEN_LAST[0:TM, :], mix_w1[:, 4 * TM:5 * TM], mixed_x[:], start=True, stop=True).then_inc(s_hidden, 1)
                        pe.wait_ge(s_hidden_out, n + 1)
                        pe.wait_ge(s_params, 1)
                        for f in range(5):
                            m = 5 * n + f
                            if m >= 2:
                                pe.wait_ge(s_mix_out, m - 1)
                            rows = slice(TM * f, TM * f + TM)
                            w2, hid = (mix_w2[rows, :], mix_hidden[rows, :]) if f < 4 else (mix_w2_last[:], mix_hidden_last[:])
                            pe.matmul(bank[MIX[m % 2]], w2, hid, start=True, stop=True).then_inc(s_mix, 1)
                    elif s[0] == "project":
                        pe.wait_ge(s_mixed, 5 * n + 1)
                        product(("decay1", n), decay_w1[:], mixed[:, par, 0, :], TD)
                        pe.wait_ge(s_dhidden, n + 1)
                        product(("decay2", n), decay_w2[:], decay_hidden[:])
                        pe.wait_ge(s_mixed, 5 * n + 5)
                        product(("r", n), w_time[:, W_R, :], mixed[:, par, 3, :])
                        product(("k", n), w_time[:, W_K, :], mixed[:, par, 1, :])
                        product(("v", n), w_time[:, W_V, :], mixed[:, par, 2, :])
                        product(("g", n), w_time[:, W_G, :], mixed[:, par, 4, :])
                        pe.wait_ge(s_bonus_in, n + 1)
                        product(("bonus", n), same_head[:], bonus_in[:])
                    elif s[0] == "state":
                        j = s[2]
                        pe.wait_ge(s_vweight, 1)
                        product(s, v_weight[:, j, :], mixed[:, par, 2, :])
                        q = D * n + j
                        if j:
                            pe.wait_ge(s_tocolumn, 1)
                            pe.wait_ge(s_read, q)
                            if j == 1 and n:
                                pe.wait_ge(s_y_sum, n)
                            pe.matmul(Y, to_column[:, j - 1, :], read[:, (q - 1) % 2], start=(j == 1), stop=False).then_inc(s_y, 1)
                    elif s[0] == "sum":
                        q = D * n + D
                        pe.wait_ge(s_read, q)
                        pe.matmul(Y, to_column[:, D - 1, :], read[:, (q - 1) % 2], start=False, stop=True).then_inc(s_y, 1)
                    elif s[0] == "mean":
                        pe.wait_ge(s_y_sum, n + 1)
                        if n:
                            pe.wait_ge(s_x2, n)
                        pe.matmul(POST, same_head_mean[:], y_sum[:], start=True, stop=True).then_inc(s_mean, 1)
                    elif s[0] == "variance":
                        pe.wait_ge(s_y_sq, n + 1)
                        pe.wait_ge(s_y_cen, n + 1)
                        pe.matmul(POST, same_head_mean[:], y_sq[:], start=True, stop=True).then_inc(s_var, 1)
                    elif s[0] == "output":
                        pe.wait_ge(s_y_var, n + 1)
                        pe.wait_ge(s_y_gated, n + 1)
                        for k in range(TPB):
                            last = pe.matmul(POST[:, C * k:C * k + C], y_gated[:, P * k:P * k + P], w_time[:, W_O, :],
                                             start=True, stop=True)
                        last.then_inc(s_out, 1)

            @block.vector
            def _(v):
                ln_vector(v, 1)
                v.wait_ge(s_params, 1)
                for s in order:
                    n = s[1]
                    par = n % 2
                    cols = slice(BLK * n, BLK * n + BLK)
                    if s[0] == "mix":
                        v.wait_ge(s_ln_T, NB + n + 1)
                        x = ln_T[:, cols].rearrange(SEQ, n=N)
                        dx = diff[:, par].rearrange(SEQ, n=N)
                        if n >= 2:
                            v.wait_ge(s_mix_out, 5 * (n - 1))
                        nc.vector.tensor_tensor(dx[:, :, 1:N], x[:, :, 0:N - 1], x[:, :, 1:N], ALU.subtract)
                        nc.vector.tensor_scalar(dx[:, :, 0:1], x[:, :, 0:1], -1.0, None, ALU.mult).then_inc(s_diff, 1)
                        v.wait_ge(s_diff, n + 1)
                        if n:
                            v.wait_ge(s_hidden, n)
                        nc.vector.scalar_tensor_tensor(mixed_x[:], diff[:, par], params[:, PAR_X:PAR_X + 1],
                                                       ln_T[:, cols], ALU.mult, ALU.add).then_inc(s_mixed_x, 1)
                        for f, k in enumerate((PAR_W, PAR_K, PAR_V, PAR_R, PAR_G)):
                            m = 5 * n + f
                            v.wait_ge(s_mix, m + 1)
                            if m >= 2:
                                v.wait_ge(s_mixed, m - 1)
                            nc.vector.scalar_tensor_tensor(mix_part[:, m % 2, :], bank[MIX[m % 2]], params[:, k:k + 1],
                                                           diff[:, par], ALU.add, ALU.mult).then_inc(s_mix_out, 1)
                    elif s[0] == "project":
                        v.wait_ge(s_recep, n + 1)
                        v.wait_ge(s_key, n + 1)
                        if n:
                            v.wait_ge(s_bonus, n)
                        nc.vector.scalar_tensor_tensor(bonus_in[:], recep[:, par], params[:, PAR_BONUS:PAR_BONUS + 1],
                                                       key[:, par], ALU.mult, ALU.mult).then_inc(s_bonus_in, 1)
                        v.wait_ge(s_prod, prod_no[("bonus", n)] + 1)
                        v.wait_ge(s_value, n + 1)
                        if n >= 2:
                            v.wait_ge(s_y_sum, n - 1)
                        nc.vector.tensor_tensor(bonus[:, par], prod_bank(("bonus", n)), value[:], ALU.mult).then_inc(s_bonus, 1)
                    elif s[0] == "state":
                        q = D * n + s[2]
                        v.wait_ge(s_prod, prod_no[s] + 1)
                        if q >= 2:
                            v.wait_ge(s_state, q - 1)
                        nc.vector.tensor_tensor(kv[:, q % 2], prod_bank(s), key[:, par], ALU.mult).then_inc(s_kv, 1)
                        v.wait_ge(s_kv, q + 1)
                        v.wait_ge(s_decay_cut, n + 1)
                        if q >= 2:
                            v.wait_ge(s_read, q - 1)
                        nc.vector.tensor_tensor_scan(state[:, q % 2], decay[:, par], kv[:, q % 2], 0.0,
                                                     ALU.mult, ALU.add).then_inc(s_state, 1)
                    elif s[0] == "sum":
                        v.wait_ge(s_y, D * n + D)
                        v.wait_ge(s_bonus, n + 1)
                        if n:
                            v.wait_ge(s_y_cen, n)
                        nc.vector.tensor_tensor(y_sum[:], Y, bonus[:, par], ALU.add).then_inc(s_y_sum, 1)
                    elif s[0] == "mean":
                        v.wait_ge(s_mean, n + 1)
                        v.wait_ge(s_y_sum, n + 1)
                        if n:
                            v.wait_ge(s_y_norm, n)
                        nc.vector.tensor_tensor(y_cen[:], y_sum[:], POST, ALU.subtract).then_inc(s_y_cen, 1)
                    elif s[0] == "variance":
                        v.wait_ge(s_var, n + 1)
                        if n:
                            v.wait_ge(s_y_invvar, n)
                        nc.vector.tensor_scalar(y_var[:], POST, GN_EPS, None, ALU.add).then_inc(s_y_var, 1)
                        v.wait_ge(s_y_var, n + 1)
                        if n:
                            v.wait_ge(s_y_rstd, n)
                        nc.vector.reciprocal(y_invvar[:], y_var[:]).then_inc(s_y_invvar, 1)
                    elif s[0] == "output":
                        v.wait_ge(s_y_norm, n + 1)
                        if n:
                            v.wait_ge(s_y_gated, n)
                        nc.vector.tensor_scalar(y_affine[:], y_norm[:], params[:, PAR_LN_W:PAR_LN_W + 1],
                                                params[:, PAR_LN_B:PAR_LN_B + 1], ALU.mult, ALU.add).then_inc(s_y_affine, 1)
                        v.wait_ge(s_out, n + 1)
                        tiles = slice(TPB * n, TPB * n + TPB)
                        nc.vector.tensor_tensor(x_res[:, tiles, :], x_res[:, tiles, :],
                                                POST.rearrange("p (t c) -> p t c", c=C), ALU.add).then_inc(s_x2, 1)


        with ExitStack() as scope:
            def tile(name, shape):
                return sb(name, shape, scope)

            logits = tile("logits", [P, NT, E])
            rank = tile("rank", [P, E])
            best = tile("best", [P, NT])
            is_best = tile("is_best", [P, NT, E])
            best_rank = tile("best_rank", [P, NT])
            first_hot = tile("first_hot", [P, NT, E])
            others = tile("others", [P, NT, E])
            second = tile("second", [P, NT])
            is_second = tile("is_second", [P, NT, E])
            second_rank = tile("second_rank", [P, NT])
            second_hot = tile("second_hot", [P, NT, E])
            gap = tile("gap", [P, NT])
            gap_exp = tile("gap_exp", [P, NT])
            gap_den = tile("gap_den", [P, NT])
            prob_first = tile("prob_first", [P, NT])
            prob_second = tile("prob_second", [P, NT])
            share_first = tile("share_first", [P, NT, E])
            share_second = tile("share_second", [P, NT, E])
            combine = tile("combine", [P, NT, E])
            silu = tile("silu", [P, 2, BLK])
            hidden = tile("hidden", [P, 2, len(expert_chunks(I)), BLK])

            s_logits = sem("s_logits")
            s_logits_out = sem("s_logits_out")
            s_rank = sem("s_rank")
            s_top = sem("s_top")
            s_gap_exp = sem("s_gap_exp")
            s_up = sem("s_up")
            s_silu = sem("s_silu")
            s_hidden_done = sem("s_hidden_done")
            s_down = sem("s_down")
            s_acc = sem("s_acc")
            s_stored = sem("s_stored")

            GATE_BANK, UP_BANK, DOWN_BANK = (0, 1), (2, 3), (4, 5)
            experts = [(e, expert_chunks(I)) for e in range(E)] + [(E, expert_chunks(IS))]
            NEX = len(experts)
            pieces = [(e, k, start, size) for e, chunks in experts for k, (start, size) in enumerate(chunks)]
            NPIECE = len(pieces)
            assert NPIECE % 2 == 0
            last_piece = {e: q for q, (e, _, _, _) in enumerate(pieces)}

            TOP_GAP = 9

            def over_blocks(eng, body):
                body(0)
                with eng.Fori(1, NB) as n:
                    body(n)

            def later(n, q):
                return q >= 2 or not isinstance(n, int)

            block = scope.enter_context(nc.Block())

            @block.sync
            def _(sp):
                for n in range(NB):
                    sp.wait_ge(s_acc, NEX * (n + 1))
                    tiles = slice(TPB * n, TPB * n + TPB)
                    sp.dma_start(out_tiles[:, tiles, :], x_res[:, tiles, :]).then_inc(s_stored, 16)
                sp.wait_ge(s_stored, 16 * NB)

            @block.gpsimd
            def _(pool):
                for e in range(E):
                    last = nc.gpsimd.memset(rank[:, e:e + 1], float(E - e))
                last.then_inc(s_rank, 1)
                ln_gpsimd(pool, 2)

            @block.scalar
            def _(act):
                ln_scalar_square(act, 2)
                ln_scalar_evacuate(act, 2, (6, 7))
                act.wait_ge(s_logits, 1)
                nc.scalar.copy(logits[:].rearrange("p t e -> p (t e)"), bank[6][:, 0:NT * E]).then_inc(s_logits_out, 1)
                act.wait_ge(s_top, TOP_GAP)
                nc.scalar.activation(gap_exp[:], gap[:], ACT.Exp).then_inc(s_gap_exp, 1)

                def body(n):
                    for q, (e, k, start, size) in enumerate(pieces):
                        act.wait_ge(s_up, NPIECE * n + (q + 1))
                        if later(n, q):
                            act.wait_ge(s_hidden_done, NPIECE * n + (q - 1))
                        nc.scalar.activation(silu[0:size, q % 2, :], bank[GATE_BANK[q % 2]][0:size], ACT.Silu).then_inc(s_silu, 1)

                over_blocks(act, body)

            @block.tensor
            def _(pe):
                ln_tensor(pe, 2, (6, 7))
                pe.wait_ge(s_ln_T, 3 * NB)
                for k in range(NT):
                    last = pe.matmul(bank[6][:, E * k:E * k + E], ln_T[:, P * k:P * k + P], gate_w[:], start=True, stop=True)
                last.then_inc(s_logits, 1)
                pe.wait_ge(s_ffn_w_in, 16 * FFN_W_DMAS)

                def down(n, e, chunks):
                    pe.wait_ge(s_hidden_done, NPIECE * n + (last_piece[e] + 1))
                    if later(n, e):
                        pe.wait_ge(s_acc, NEX * n + (e - 1))
                    for k in range(TPB):
                        for c, (start, size) in enumerate(chunks):
                            w = w_down[0:size, e, c, :] if e < E else ws_down[0:size, c, :]
                            last = pe.matmul(bank[DOWN_BANK[e % 2]][:, C * k:C * k + C],
                                             hidden[0:size, e % 2, c, P * k:P * k + P], w,
                                             start=(c == 0), stop=(c == len(chunks) - 1))
                    last.then_inc(s_down, 1)

                def body(n):
                    x = ln_T[:, bass.ds(n * BLK, BLK)]
                    for e, chunks in experts:
                        for q, (e_, k, start, size) in enumerate(pieces):
                            if e_ != e:
                                continue
                            if later(n, q):
                                pe.wait_ge(s_hidden_done, NPIECE * n + (q - 1))
                            wg = w_gate[:, e, start:start + size] if e < E else ws_gate[:, start:start + size]
                            wu = w_up[:, e, start:start + size] if e < E else ws_up[:, start:start + size]
                            pe.matmul(bank[GATE_BANK[q % 2]][0:size], wg, x, start=True, stop=True)
                            pe.matmul(bank[UP_BANK[q % 2]][0:size], wu, x, start=True, stop=True).then_inc(s_up, 1)
                        if e:
                            down(n, *experts[e - 1])
                    down(n, *experts[-1])

                over_blocks(pe, body)

            @block.vector
            def _(v):
                ln_vector(v, 2)
                done = [0]

                def step(ins):
                    done[0] += 1
                    ins.then_inc(s_top, 1)
                    v.wait_ge(s_top, done[0])

                def over_experts(a):
                    return a[:].unsqueeze(2).broadcast_to([P, NT, E])

                ranks = rank[:].unsqueeze(1).broadcast_to([P, NT, E])
                v.wait_ge(s_logits_out, 1)
                v.wait_ge(s_rank, 1)
                step(nc.vector.tensor_reduce(best[:], logits[:], AX.X, ALU.max))
                step(nc.vector.tensor_tensor(is_best[:], logits[:], over_experts(best), ALU.is_equal))
                step(nc.vector.tensor_tensor(is_best[:], is_best[:], ranks, ALU.mult))
                step(nc.vector.tensor_reduce(best_rank[:], is_best[:], AX.X, ALU.max))
                step(nc.vector.tensor_tensor(first_hot[:], is_best[:], over_experts(best_rank), ALU.is_equal))
                step(nc.vector.scalar_tensor_tensor(others[:], first_hot[:], -3e38, logits[:], ALU.mult, ALU.add))
                step(nc.vector.tensor_reduce(second[:], others[:], AX.X, ALU.max))
                step(nc.vector.tensor_tensor(is_second[:], others[:], over_experts(second), ALU.is_equal))
                step(nc.vector.tensor_tensor(gap[:], second[:], best[:], ALU.subtract))
                step(nc.vector.tensor_tensor(is_second[:], is_second[:], ranks, ALU.mult))
                step(nc.vector.tensor_reduce(second_rank[:], is_second[:], AX.X, ALU.max))
                step(nc.vector.tensor_tensor(second_hot[:], is_second[:], over_experts(second_rank), ALU.is_equal))
                v.wait_ge(s_gap_exp, 1)
                step(nc.vector.tensor_scalar(gap_den[:], gap_exp[:], 1.0, None, ALU.add))
                step(nc.vector.reciprocal(prob_first[:], gap_den[:]))
                step(nc.vector.tensor_tensor(prob_second[:], gap_exp[:], prob_first[:], ALU.mult))
                step(nc.vector.tensor_tensor(share_first[:], first_hot[:], over_experts(prob_first), ALU.mult))
                step(nc.vector.tensor_tensor(share_second[:], second_hot[:], over_experts(prob_second), ALU.mult))
                step(nc.vector.tensor_tensor(combine[:], share_first[:], share_second[:], ALU.add))

                def accumulate(n, e):
                    v.wait_ge(s_down, NEX * n + (e + 1))
                    if not (isinstance(n, int) and e == 0):
                        v.wait_ge(s_acc, NEX * n + e)
                    out_bank = bank[DOWN_BANK[e % 2]]
                    if e < E:
                        for k in range(TPB):
                            row = x_res[:, bass.ds(n * TPB + k, 1), :].rearrange("p a c -> p (a c)")
                            share = combine[:, bass.ds(n * TPB + k, 1), e:e + 1].rearrange("p a e -> p (a e)")
                            last = nc.vector.scalar_tensor_tensor(row, out_bank[:, C * k:C * k + C], share, row, ALU.mult, ALU.add)
                    else:
                        rows = x_res[:, bass.ds(n * TPB, TPB), :]
                        last = nc.vector.tensor_tensor(rows, out_bank.rearrange("p (t c) -> p t c", c=C), rows, ALU.add)
                    last.then_inc(s_acc, 1)

                def body(n):
                    for e, chunks in experts:
                        for q, (e_, k, start, size) in enumerate(pieces):
                            if e_ != e:
                                continue
                            v.wait_ge(s_silu, NPIECE * n + (q + 1))
                            if k == 0 and later(n, e):
                                v.wait_ge(s_down, NEX * n + (e - 1))
                            nc.vector.tensor_tensor(hidden[0:size, e % 2, k, :], silu[0:size, q % 2, :],
                                                    bank[UP_BANK[q % 2]][0:size], ALU.mult).then_inc(s_hidden_done, 1)
                        if e:
                            accumulate(n, e - 1)
                    accumulate(n, E)

                over_blocks(v, body)


_INS = ['x', 'ctx_2048', 'L0_xattn_w_qkv', 'L0_xattn_w_proj', 'L0_xattn_b_proj',
        'L0_attn_time_maa_x', 'L0_attn_time_maa_w', 'L0_attn_time_maa_k', 'L0_attn_time_maa_v',
        'L0_attn_time_maa_r', 'L0_attn_time_maa_g', 'L0_attn_time_maa_w1', 'L0_attn_time_maa_w2',
        'L0_attn_time_decay', 'L0_attn_time_decay_w1', 'L0_attn_time_decay_w2', 'L0_attn_time_faaaa',
        'L0_attn_W_r', 'L0_attn_W_k', 'L0_attn_W_v', 'L0_attn_W_g', 'L0_attn_W_o',
        'L0_attn_ln_w', 'L0_attn_ln_b', 'L0_ffn_gate_w', 'L0_ffn_Wg', 'L0_ffn_Wu', 'L0_ffn_Wd',
        'L0_ffn_Sg', 'L0_ffn_Su', 'L0_ffn_Sd']


def kernel(**inputs):
    import numpy as _np
    import concourse.bacc as _bacc
    from concourse import mybir as _mybir
    from concourse.bass_utils import run_bass_kernel_spmd as _run

    nc = _bacc.Bacc("TRN2", target_bir_lowering=False, num_devices=1)
    arrays, handles = {}, {}
    for name in _INS:
        a = _np.ascontiguousarray(inputs[name])
        arrays[f"in_{name}"] = a
        handles[name] = nc.dram_tensor(f"in_{name}", a.shape, _mybir.dt.from_np(a.dtype), kind="ExternalInput").ap()
    out = nc.dram_tensor("out_0", (B, N, C), F32, kind="ExternalOutput").ap()
    perceiver_layer(nc, handles, out)
    r = _run(nc, [arrays], core_ids=[0])
    return r.results[0]["out_0"]
```

```python
from contextlib import ExitStack

import concourse.bass as bass
from concourse import mybir

F32 = mybir.dt.float32
F32R = mybir.dt.float32r
ALU = mybir.AluOpType
ACT = mybir.ActivationFunctionType
AX = mybir.AxisListType

P = 128
C = 128
B = 64
N = 32
NT = B * N // P
BLK = 512
NB = B * N // BLK
TPB = BLK // P
SPB = BLK // N
H = 16
D = C // H
G = 4
HG = H // G
NCTX = 257
KC = 2
KEYS = NCTX + N
LN_EPS = 1e-5
GN_EPS = 1e-5 * 64
TM = 32
TD = 64
E = 8
I = 352
IS = 176
PAR_X, PAR_W, PAR_K, PAR_V, PAR_R, PAR_G, PAR_DECAY, PAR_BONUS, PAR_LN_W, PAR_LN_B = range(10)
NPAR = 10
W_R, W_K, W_V, W_G, W_O = range(5)


TIME_W_DMAS = 20
FFN_W_DMAS = 10


def expert_chunks(width):
    n = -(-width // P)
    size = -(-width // (16 * n)) * 16
    return [(s, min(size, width - s)) for s in range(0, width, size)]


def perceiver_layer(nc, t, out):
    x_tiles = t["x"].rearrange("b n c -> (b n) c").rearrange("(t p) c -> p t c", p=P)
    out_tiles = out.rearrange("b n c -> (b n) c").rearrange("(t p) c -> p t c", p=P)
    ctx_dram = t["ctx_2048"]

    with ExitStack() as whole:
        def sem(name):
            return whole.enter_context(nc.semaphore(name))

        def sb(name, shape, scope=whole):
            return scope.enter_context(nc.sbuf_tensor(name, shape, F32))

        psum = whole.enter_context(nc.psum_tensor("psum", [P, 8, BLK], F32))
        bank = [psum[:, i, :] for i in range(8)]

        x_res = sb("x_res", [P, NT, C])
        x_cen = sb("x_cen", [P, NT, C])
        x_sq = sb("x_sq", [P, NT, C])
        ln_T = sb("ln_T", [P, B * N])
        ln_sum = sb("ln_sum", [P, NT])
        ln_negmean = sb("ln_negmean", [P, NT])
        ln_sqsum = sb("ln_sqsum", [P, NT])
        ln_var = sb("ln_var", [P, NT])
        ln_rstd = sb("ln_rstd", [P, NT])
        minus_half = sb("minus_half", [P, NT])
        ones = sb("ones", [P, G])
        ident = sb("ident", [P, P])
        head_of = sb("head_of", [P, H])
        quad_of = sb("quad_of", [P, G])
        same_head = sb("same_head", [P, P])
        same_head_mean = sb("same_head_mean", [P, P])

        mix_w1 = sb("mix_w1", [P, 5 * TM])
        mix_w2 = sb("mix_w2", [P, C])
        mix_w2_last = sb("mix_w2_last", [TM, C])
        decay_w1 = sb("decay_w1", [P, TD])
        decay_w2 = sb("decay_w2", [TD, C])
        w_time = sb("w_time", [P, 5, C])
        param_rows = sb("param_rows", [NPAR, C])
        gate_w = sb("gate_w", [P, E])
        w_gate = sb("w_gate", [P, E, I])
        w_up = sb("w_up", [P, E, I])
        w_down = sb("w_down", [P, E, len(expert_chunks(I)), C])
        ws_gate = sb("ws_gate", [P, IS])
        ws_up = sb("ws_up", [P, IS])
        ws_down = sb("ws_down", [P, len(expert_chunks(IS)), C])

        s_time_w_in = sem("s_time_w_in")
        s_ffn_w_in = sem("s_ffn_w_in")
        s_x_in = [sem(f"s_x_in{i}") for i in range(NB)]
        s_ln_sum = sem("s_ln_sum")
        s_ln_negmean = sem("s_ln_negmean")
        s_ln_cen = sem("s_ln_cen")
        s_ln_sq = sem("s_ln_sq")
        s_ln_sqsum = sem("s_ln_sqsum")
        s_ln_var = sem("s_ln_var")
        s_ln_rstd = sem("s_ln_rstd")
        s_ln_norm = sem("s_ln_norm")
        s_ln_turned = sem("s_ln_turned")
        s_ln_T = sem("s_ln_T")
        s_const = sem("s_const")

        def ln_vector(v, which, x_ready=None):
            at = NB * which

            def centre(n):
                tiles = slice(TPB * n, TPB * n + TPB)
                if x_ready:
                    x_ready(n)
                nc.vector.tensor_reduce(ln_sum[:, tiles], x_res[:, tiles, :], AX.X, ALU.add).then_inc(s_ln_sum, 1)
                v.wait_ge(s_ln_sum, at + n + 1)
                nc.vector.tensor_scalar(ln_negmean[:, tiles], ln_sum[:, tiles], -1.0 / C, None, ALU.mult).then_inc(s_ln_negmean, 1)
                v.wait_ge(s_ln_negmean, at + n + 1)
                nc.vector.tensor_tensor(x_cen[:, tiles, :], x_res[:, tiles, :],
                                        ln_negmean[:, tiles].unsqueeze(2).broadcast_to([P, TPB, C]),
                                        ALU.add).then_inc(s_ln_cen, 1)

            def variance(n):
                tiles = slice(TPB * n, TPB * n + TPB)
                v.wait_ge(s_ln_sq, at + n + 1)
                nc.vector.tensor_reduce(ln_sqsum[:, tiles], x_sq[:, tiles, :], AX.X, ALU.add).then_inc(s_ln_sqsum, 1)
                v.wait_ge(s_ln_sqsum, at + n + 1)
                nc.vector.tensor_scalar(ln_var[:, tiles], ln_sqsum[:, tiles], 1.0 / C, LN_EPS,
                                        ALU.mult, ALU.add).then_inc(s_ln_var, 1)

            def normalise_rows(n):
                tiles = slice(TPB * n, TPB * n + TPB)
                v.wait_ge(s_ln_rstd, at + n + 1)
                nc.vector.tensor_tensor(x_cen[:, tiles, :], x_cen[:, tiles, :],
                                        ln_rstd[:, tiles].unsqueeze(2).broadcast_to([P, TPB, C]),
                                        ALU.mult).then_inc(s_ln_norm, 1)

            centre(0)
            for n in range(NB):
                if n + 1 < NB:
                    centre(n + 1)
                variance(n)
                if n:
                    normalise_rows(n - 1)
            normalise_rows(NB - 1)

        def ln_scalar_square(act, which, blocks):
            for n in blocks:
                tiles = slice(TPB * n, TPB * n + TPB)
                act.wait_ge(s_ln_cen, NB * which + n + 1)
                nc.scalar.activation(x_sq[:, tiles, :], x_cen[:, tiles, :], ACT.Square).then_inc(s_ln_sq, 1)

        def ln_scalar_evacuate(act, which, banks, blocks):
            for n in blocks:
                act.wait_ge(s_ln_turned, NB * which + n + 1)
                nc.scalar.copy(ln_T[:, BLK * n:BLK * n + BLK], bank[banks[n % 2]][:]).then_inc(s_ln_T, 1)

        def ln_gpsimd(pool, which):
            for n in range(NB):
                tiles = slice(TPB * n, TPB * n + TPB)
                pool.wait_ge(s_ln_var, NB * which + n + 1)
                nc.gpsimd.tensor_tensor(ln_rstd[:, tiles], ln_var[:, tiles], minus_half[:, tiles],
                                        ALU.pow).then_inc(s_ln_rstd, 1)

        def ln_tensor(pe, which, banks):
            for n in range(NB):
                pe.wait_ge(s_ln_norm, NB * which + n + 1)
                if n >= 2:
                    pe.wait_ge(s_ln_T, NB * which + n - 1)
                for k in range(TPB):
                    last = pe.transpose(bank[banks[n % 2]][:, P * k:P * k + P], x_cen[:, TPB * n + k, :], ident[:])
                last.then_inc(s_ln_turned, 1)

        with ExitStack() as scope:
            NSLOT = 4
            w_rows = sb("w_rows", [P, 4, C], scope)
            w_T = sb("w_T", [P, 4, C], scope)
            b_rows = sb("b_rows", [P, C], scope)
            qT = sb("qT", [P, B * N], scope)
            k_own = sb("k_own", [P, B, N + 1], scope)
            v_own = sb("v_own", [P, B, C // G], scope)
            k_left = sb("k_left", [B, C], scope)
            attn_T = sb("attn_T", [P, B * N], scope)
            kv_in = sb("kv_in", [P, NSLOT, KC, 2 * C], scope)
            v_left_in = sb("v_left_in", [G, NSLOT, C], scope)
            q_heads = sb("q_heads", [P, 2, H, N], scope)
            kT = sb("kT", [P, 2, KEYS], scope)
            probs = sb("probs", [P, 2, G, KEYS], scope)
            probs_own = sb("probs_own", [P, 2, G, N], scope)
            probs_left = sb("probs_left", [P, 2, G], scope)
            neg_max = sb("neg_max", [P, 2, G], scope)
            row_sum = sb("row_sum", [P, 2, G], scope)
            inv_sum = sb("inv_sum", [P, 2, G], scope)
            pT = sb("pT", [P, 2, 2, BLK], scope)
            pT_own = sb("pT_own", [P, 2, P], scope)
            pT_left = sb("pT_left", [G, 2, P], scope)
            v_own_diag = sb("v_own_diag", [P, 2, C], scope)
            v_left_diag = sb("v_left_diag", [G, 2, C], scope)
            inv_spread = sb("inv_spread", [P, 2, C], scope)
            o_masked = sb("o_masked", [P, HG, N], scope)
            o_sum = sb("o_sum", [P, N], scope)
            head_in_group = sb("head_in_group", [P, HG], scope)
            head_scaled = sb("head_scaled", [P, H], scope)
            query_of = sb("query_of", [P, N], scope)

            s_w_in = sem("s_w_in")
            s_kleft_in = sem("s_kleft_in")
            s_masks = sem("s_masks")
            s_masks_dve = sem("s_masks_dve")
            s_w_turned = sem("s_w_turned")
            s_w_T = sem("s_w_T")
            s_proj = sem("s_proj")
            s_qT = sem("s_qT")
            s_k_own = sem("s_k_own")
            s_v_own = sem("s_v_own")
            s_ctx_in = [sem(f"s_ctx_in{i}") for i in range(NSLOT)]
            s_ready_q = sem("s_ready_q")
            s_ready_v = sem("s_ready_v")
            s_spread = sem("s_spread")
            s_scores = sem("s_scores")
            s_max = sem("s_max")
            s_exp = sem("s_exp")
            s_probs_own = sem("s_probs_own")
            s_pT = sem("s_pT")
            s_pT_out = sem("s_pT_out")
            s_keys = sem("s_keys")
            s_keys_out = sem("s_keys_out")
            s_inv = sem("s_inv")
            s_pv = sem("s_pv")
            s_o_masked = sem("s_o_masked")
            s_o_sum = sem("s_o_sum")
            s_attn = sem("s_attn")
            s_proj_out = sem("s_proj_out")
            s_proj_bias = sem("s_proj_bias")
            s_x1 = sem("s_x1")

            S_BANK = [(0, 1), (2, 3)]
            PT_BANK = [4, 5]
            KEY_BANK = bank[6]
            O_BANK = bank[7]
            own = slice(NCTX - 1, NCTX - 1 + N)

            def over_sequences(eng, step):
                for u in range(NSLOT):
                    step(u, u)
                with eng.Fori(1, B // NSLOT - 1) as turn:
                    for u in range(NSLOT):
                        step(turn * NSLOT + u, u)
                for u in range(NSLOT):
                    step(B - NSLOT + u, u)

            def loaded(b, u):
                return b * (32 // NSLOT) + (32 - u * (32 // NSLOT))

            def queries_of(b):
                return bass.ds(b * N, N)

            def first(b, n):
                return isinstance(b, int) and b < n

            block = scope.enter_context(nc.Block())

            @block.sync
            def _(sp):
                for n in range(NB):
                    sp.dma_start(x_res[:, TPB * n:TPB * n + TPB, :], x_tiles[:, TPB * n:TPB * n + TPB, :]).then_inc(s_x_in[n], 16)
                sp.dma_start(w_rows[:, 0:3, :], t["L0_xattn_w_qkv"].rearrange("(s o) c -> o s c", s=3)).then_inc(s_w_in, 16)
                sp.dma_start(w_rows[:, 3, :], t["L0_xattn_w_proj"]).then_inc(s_w_in, 16)
                sp.dma_start(b_rows[:], t["L0_xattn_b_proj"].rearrange("(a c) -> a c", a=1).broadcast_to([P, C])).then_inc(s_w_in, 16)
                sp.dma_start(k_left[:], ctx_dram[:, NCTX - 1, 0:C]).then_inc(s_kleft_in, 16)

                def load(b, u):
                    if not first(b, NSLOT):
                        sp.wait_ge(s_pv, b - NSLOT + 1)
                        sp.wait_ge(s_ready_v, b - NSLOT + 1)
                    sp.dma_start(kv_in[:, u, :, :], ctx_dram[bass.ds(b, 1), 0:NCTX - 1, :].rearrange(
                        "a (p c) d -> p (a c) d", c=KC)).then_inc(s_ctx_in[u], 16)
                    sp.dma_start(v_left_in[:, u, :], ctx_dram[bass.ds(b, 1), NCTX - 1, C:2 * C].broadcast_to([G, C])
                                 ).then_inc(s_ctx_in[u], 16)

                for u in range(NSLOT):
                    load(u, u)
                sp.dma_start(mix_w1[:], t["L0_attn_time_maa_w1"]).then_inc(s_time_w_in, 16)
                mix_w2_rows = t["L0_attn_time_maa_w2"].rearrange("f e c -> (f e) c")
                sp.dma_start(mix_w2[:], mix_w2_rows[0:4 * TM, :]).then_inc(s_time_w_in, 16)
                sp.dma_start(mix_w2_last[:], mix_w2_rows[4 * TM:5 * TM, :]).then_inc(s_time_w_in, 16)
                sp.dma_start(decay_w1[:], t["L0_attn_time_decay_w1"]).then_inc(s_time_w_in, 16)
                sp.dma_start(decay_w2[:], t["L0_attn_time_decay_w2"]).then_inc(s_time_w_in, 16)
                for k, name in enumerate(["W_r", "W_k", "W_v", "W_g", "W_o"]):
                    sp.dma_start(w_time[:, k, :], t["L0_attn_" + name]).then_inc(s_time_w_in, 16)
                for k, name in enumerate(["time_maa_x", "time_maa_w", "time_maa_k", "time_maa_v", "time_maa_r",
                                          "time_maa_g", "time_decay"]):
                    sp.dma_start(param_rows[k:k + 1, :], t["L0_attn_" + name].rearrange("a b c -> (a b) c")).then_inc(s_time_w_in, 16)
                sp.dma_start(param_rows[PAR_BONUS:PAR_BONUS + 1, :],
                             t["L0_attn_time_faaaa"].rearrange("(a h) d -> a (h d)", a=1)).then_inc(s_time_w_in, 16)
                for k, name in ((PAR_LN_W, "ln_w"), (PAR_LN_B, "ln_b")):
                    sp.dma_start(param_rows[k:k + 1, :], t["L0_attn_" + name].rearrange("(a c) -> a c", a=1)).then_inc(s_time_w_in, 16)
                def expert_weights(turn):
                    if turn == 1:
                        sp.dma_start(w_gate[:], t["L0_ffn_Wg"].rearrange("e h i -> h e i")).then_inc(s_ffn_w_in, 16)
                    elif turn == 2:
                        sp.dma_start(w_up[:], t["L0_ffn_Wu"].rearrange("e h i -> h e i")).then_inc(s_ffn_w_in, 16)
                    elif turn == 3:
                        for k, (start, size) in enumerate(expert_chunks(I)):
                            sp.dma_start(w_down[0:size, :, k, :],
                                         t["L0_ffn_Wd"][:, start:start + size, :].rearrange("e i c -> i e c")).then_inc(s_ffn_w_in, 16)
                    else:
                        sp.dma_start(gate_w[:], t["L0_ffn_gate_w"]).then_inc(s_ffn_w_in, 16)
                        sp.dma_start(ws_gate[:], t["L0_ffn_Sg"]).then_inc(s_ffn_w_in, 16)
                        sp.dma_start(ws_up[:], t["L0_ffn_Su"]).then_inc(s_ffn_w_in, 16)
                        for k, (start, size) in enumerate(expert_chunks(IS)):
                            sp.dma_start(ws_down[0:size, k, :], t["L0_ffn_Sd"][start:start + size, :]).then_inc(s_ffn_w_in, 16)

                TURNS_WITH_WEIGHTS = 4
                for turn in range(1, TURNS_WITH_WEIGHTS + 1):
                    for u in range(NSLOT):
                        load(turn * NSLOT + u, u)
                    expert_weights(turn)
                with sp.Fori(TURNS_WITH_WEIGHTS + 1, B // NSLOT) as turn:
                    for u in range(NSLOT):
                        load(turn * NSLOT + u, u)

            @block.gpsimd
            def _(pool):
                g = nc.gpsimd
                made = [0]

                def link(ins):
                    made[0] += 1
                    ins.then_inc(s_const, 1)
                    pool.wait_ge(s_const, made[0])

                g.memset(minus_half[:], -0.5)
                g.memset(ones[:], 1.0)
                g.memset(head_of[:], 1.0)
                g.memset(quad_of[:], 1.0)
                link(g.memset(ident[:], 0.0))
                g.affine_select(out=ident[:], in_=ident[:], compare_op=ALU.not_equal, fill=1.0, base=0,
                                pattern=[[-1, P]], channel_multiplier=1)
                g.affine_select(out=head_of[:], in_=head_of[:], compare_op=ALU.is_ge, fill=0.0, base=0,
                                pattern=[[-D, H]], channel_multiplier=1)
                link(g.affine_select(out=quad_of[:], in_=quad_of[:], compare_op=ALU.is_ge, fill=0.0, base=0,
                                     pattern=[[-N, G]], channel_multiplier=1))
                g.affine_select(out=head_of[:], in_=head_of[:], compare_op=ALU.is_ge, fill=0.0, base=D - 1,
                                pattern=[[D, H]], channel_multiplier=-1)
                g.affine_select(out=quad_of[:], in_=quad_of[:], compare_op=ALU.is_ge, fill=0.0, base=N - 1,
                                pattern=[[N, G]], channel_multiplier=-1).then_inc(s_masks, 1)
                pool.wait_ge(s_masks, 1)
                g.tensor_copy(same_head[:].rearrange("p (h d) -> p h d", h=H),
                              head_of[:].unsqueeze(2).broadcast_to([P, H, D])).then_inc(s_masks, 1)
                ln_gpsimd(pool, 0)
                pool.wait_ge(s_masks_dve, 2)

                def ready_q(b, par):
                    n = b // SPB if isinstance(b, int) else None
                    if first(b, B):
                        pool.wait_ge(s_qT, n + 1)
                        pool.wait_ge(s_k_own, n + 2)
                    if not first(b, 2):
                        pool.wait_ge(s_scores, 2 * b - 2)
                    g.tensor_tensor(q_heads[:, par], qT[:, queries_of(b)].unsqueeze(1).broadcast_to([P, H, N]),
                                    head_scaled[:].unsqueeze(2).broadcast_to([P, H, N]), ALU.mult)
                    g.tensor_copy(kT[:, par, NCTX - 1:KEYS], k_own[:, bass.ds(b, 1), :].rearrange("p a n -> p (a n)")).then_inc(s_ready_q, 1)

                def ready_v(b, u, par):
                    if isinstance(b, int):
                        pool.wait_ge(s_v_own, b // SPB + 1)
                    pool.wait_ge(s_ctx_in[u], loaded(b, u))
                    if not first(b, 2):
                        pool.wait_ge(s_pv, b - 1)
                    g.tensor_tensor(v_own_diag[:, par].rearrange("p (g c) -> p g c", g=G),
                                    v_own[:, bass.ds(b, 1), :].broadcast_to([P, G, C // G]),
                                    quad_of[:].unsqueeze(2).broadcast_to([P, G, C // G]), ALU.mult)
                    g.tensor_tensor(v_left_diag[:, par].rearrange("p (g c) -> p g c", g=G),
                                    v_left_in[:, u, :].rearrange("p (g c) -> p g c", g=G),
                                    ident[0:G, 0:G].unsqueeze(2).broadcast_to([G, G, C // G]), ALU.mult).then_inc(s_ready_v, 1)

                def spread(b, par):
                    pool.wait_ge(s_inv, b + 1)
                    if not first(b, 2):
                        pool.wait_ge(s_pv, b - 1)
                    g.tensor_tensor(inv_spread[:, par].rearrange("p (g h d) -> p g h d", g=G, h=HG),
                                    quad_of[:].unsqueeze(1).unsqueeze(3).broadcast_to([P, G, HG, D]),
                                    inv_sum[:, par].unsqueeze(2).unsqueeze(3).broadcast_to([P, G, HG, D]),
                                    ALU.mult).then_inc(s_spread, 1)

                def pack_own(b, par):
                    pool.wait_ge(s_exp, 2 * b + 2)
                    if not first(b, 2):
                        pool.wait_ge(s_keys, b + 1)
                    g.tensor_tensor(probs_own[:, par], probs[:, par, :, own],
                                    ones[:].unsqueeze(2).broadcast_to([P, G, N]), ALU.mult)
                    g.tensor_copy(probs_left[:, par], probs[:, par, :, KEYS - 1]).then_inc(s_probs_own, 1)

                ready_q(0, 0)

                def step(b, u):
                    if not first(b, 1):
                        pack_own(b - 1, (u + 1) % 2)
                    if not (isinstance(b, int) and b == B - 1):
                        ready_q(b + 1, (u + 1) % 2)
                    ready_v(b, u, u % 2)
                    if not first(b, 1):
                        spread(b - 1, (u + 1) % 2)

                for u in range(NSLOT):
                    step(u, u)
                pool.wait_ge(s_qT, NB)
                pool.wait_ge(s_k_own, NB + 1)
                pool.wait_ge(s_v_own, NB)
                with pool.Fori(1, B // NSLOT - 1) as turn:
                    for u in range(NSLOT):
                        step(turn * NSLOT + u, u)
                for u in range(NSLOT):
                    step(B - NSLOT + u, u)
                pack_own(B - 1, 1)
                spread(B - 1, 1)

            @block.scalar
            def _(act):
                ln_scalar_square(act, 0, range(NB - 1))
                act.wait_ge(s_w_turned, 1)
                nc.scalar.copy(w_T[:].rearrange("p s o -> p (s o)"), bank[6][:]).then_inc(s_w_T, 1)
                act.wait_ge(s_w_turned, 2)
                nc.scalar.copy(k_own[:, :, N], bank[7][:, 0:B]).then_inc(s_k_own, 1)
                ln_scalar_evacuate(act, 0, (0, 1), [0])
                ln_scalar_square(act, 0, [NB - 1])
                ln_scalar_evacuate(act, 0, (0, 1), range(1, NB))
                for n in range(NB):
                    act.wait_ge(s_proj, 3 * n + 1)
                    nc.scalar.copy(qT[:, BLK * n:BLK * n + BLK], bank[2][:]).then_inc(s_qT, 1)
                    act.wait_ge(s_proj, 3 * n + 2)
                    nc.scalar.copy(k_own[:, SPB * n:SPB * n + SPB, 0:N],
                                   bank[3][:].rearrange("p (b n) -> p b n", n=N)).then_inc(s_k_own, 1)
                    act.wait_ge(s_proj, 3 * n + 3)
                    nc.scalar.copy(v_own[:, SPB * n:SPB * n + SPB, :].rearrange("p b c -> p (b c)"),
                                   bank[4][:]).then_inc(s_v_own, 1)

                def keys_out(b, par_keys, par_probs, lag, lead):
                    act.wait_ge(s_keys, b + 2)
                    if lag:
                        nc.scalar.copy(pT_own[:, par_probs], KEY_BANK[:, 256:384])
                        last = nc.scalar.copy(pT_left[:, par_probs], KEY_BANK[0:G, 384:512])
                    if lead:
                        last = nc.scalar.copy(kT[:, par_keys, 0:NCTX - 1], KEY_BANK[:, 0:256])
                    last.then_inc(s_keys_out, 1)

                keys_out(-1, 0, 0, False, True)

                def step(b, u):
                    par = u % 2
                    keys_out(b, (u + 1) % 2, (u + 1) % 2, not first(b, 1),
                             not (isinstance(b, int) and b == B - 1))
                    for h in range(2):
                        act.wait_ge(s_max, 2 * b + (h + 1))
                        if h == 0 and not first(b, 2):
                            act.wait_ge(s_pT, 2 * b - 2)
                            act.wait_ge(s_probs_own, b - 1)
                            act.wait_ge(s_inv, b - 1)
                        for k in range(2):
                            gr = 2 * h + k
                            last = nc.scalar.activation(probs[:, par, gr, :], bank[S_BANK[h][k]][:, 0:KEYS], ACT.Exp,
                                                        bias=neg_max[:, par, gr:gr + 1],
                                                        accum_out=row_sum[:, par, gr:gr + 1])
                        last.then_inc(s_exp, 1)

                over_sequences(act, step)
                keys_out(B, 0, 1, True, False)

            @block.tensor
            def _(pe):
                pe.wait_ge(s_w_in, 48)
                pe.wait_ge(s_masks, 1)
                for k in range(4):
                    last = pe.transpose(bank[6][:, P * k:P * k + P], w_rows[:, k, :], ident[:])
                last.then_inc(s_w_turned, 1)
                pe.wait_ge(s_kleft_in, 16)
                pe.transpose(bank[7][:, 0:B], k_left[:], ident[0:B, 0:B]).then_inc(s_w_turned, 1)
                ln_tensor(pe, 0, (0, 1))
                pe.wait_ge(s_w_T, 1)
                for n in range(NB):
                    pe.wait_ge(s_ln_T, n + 1)
                    cols = slice(BLK * n, BLK * n + BLK)
                    if n:
                        pe.wait_ge(s_qT, n)
                    pe.matmul(bank[2][:], w_T[:, 0, :], ln_T[:, cols], start=True, stop=True).then_inc(s_proj, 1)
                    if n:
                        pe.wait_ge(s_k_own, n + 1)
                    pe.matmul(bank[3][:], w_T[:, 1, :], ln_T[:, cols], start=True, stop=True).then_inc(s_proj, 1)
                    if n:
                        pe.wait_ge(s_v_own, n)
                    for k in range(SPB):
                        for gr in range(G):
                            rows = slice(N * gr, N * gr + N)
                            last = pe.matmul(bank[4][rows, N * k:N * k + C // G], ln_T[:, BLK * n + N * k:BLK * n + N * k + N],
                                             w_T[:, 2, rows], start=True, stop=True, skip_group_check=True)
                    last.then_inc(s_proj, 1)

                def keys(b, u, par_probs, lag, lead):
                    if lead:
                        pe.wait_ge(s_ctx_in[u], loaded(b + 1, u))
                        for c in range(KC):
                            last = pe.transpose(KEY_BANK[:, P * c:P * c + P], kv_in[:, u, c, 0:C], ident[:])
                    if lag:
                        pe.wait_ge(s_probs_own, b)
                        pe.transpose(KEY_BANK[:, 256:384], probs_own[:, par_probs].rearrange("p g n -> p (g n)"), ident[:])
                        last = pe.transpose(KEY_BANK[0:G, 384:512], probs_left[:, par_probs], ident[:])
                    last.then_inc(s_keys, 1)

                def turn_probs(b, par, h):
                    pe.wait_ge(s_exp, 2 * b + (h + 1))
                    if not first(b, 1):
                        pe.wait_ge(s_pT_out, 2 * b + (h - 1))
                    for k in range(2):
                        for c in range(KC):
                            last = pe.transpose(bank[PT_BANK[h]][:, P * (2 * k + c):P * (2 * k + c) + P],
                                                probs[:, par, 2 * h + k, P * c:P * c + P], ident[:])
                    last.then_inc(s_pT, 1)

                def values(b, u, par):
                    pe.wait_ge(s_ready_v, b + 1)
                    pe.wait_ge(s_keys_out, b + 3)
                    if not first(b, 1):
                        pe.wait_ge(s_attn, b)
                    pe.matmul(O_BANK[:, 0:P], v_own_diag[:, par], pT_own[:, par], start=True, stop=False, skip_group_check=True)
                    pe.matmul(O_BANK[:, 0:P], v_left_diag[:, par], pT_left[:, par], start=False, stop=False, skip_group_check=True)
                    pe.wait_ge(s_pT_out, 2 * b + 2)
                    for c in range(KC):
                        for gr in range(G):
                            rows = slice(N * gr, N * gr + N)
                            pe.matmul(O_BANK[rows, 0:P], kv_in[:, u, c, C + N * gr:C + N * gr + N],
                                      pT[:, par, gr // 2, P * (2 * (gr % 2) + c):P * (2 * (gr % 2) + c) + P],
                                      start=False, stop=(c == KC - 1), skip_group_check=True)
                    pe.wait_ge(s_spread, b + 1)
                    pe.matmul(O_BANK[:, P:P + N], inv_spread[:, par], query_of[:], start=True, stop=True,
                              skip_group_check=True).then_inc(s_pv, 1)

                keys(-1, 0, 0, False, True)
                pe.wait_ge(s_masks_dve, 2)

                def step(b, u):
                    par, before = u % 2, (u + 1) % 2
                    for h in range(2):
                        if h == 0:
                            pe.wait_ge(s_ready_q, b + 1)
                            pe.wait_ge(s_keys_out, b + 1)
                        if not first(b, 1):
                            pe.wait_ge(s_exp, 2 * b + (h - 1))
                        elif h == 0:
                            pe.wait_ge(s_k_own, NB + 1)
                            pe.wait_ge(s_v_own, NB)
                            pe.wait_ge(s_ln_T, NB)
                        for k in range(2):
                            gr = 2 * h + k
                            last = pe.matmul(bank[S_BANK[h][k]][:, 0:KEYS],
                                             q_heads[:, par, HG * gr:HG * gr + HG, :].rearrange("p h n -> p (h n)"),
                                             kT[:, par, :], start=True, stop=True)
                        last.then_inc(s_scores, 1)
                        if h == 0:
                            if not first(b, 1):
                                turn_probs(b - 1, before, 1)
                            keys(b, (u + 1) % NSLOT, before, not first(b, 1),
                                 not (isinstance(b, int) and b == B - 1))
                        else:
                            if not first(b, 1):
                                values(b - 1, (u - 1) % NSLOT, before)
                            turn_probs(b, par, 0)

                over_sequences(pe, step)
                turn_probs(B - 1, 1, 1)
                pe.wait_ge(s_keys_out, B + 1)
                keys(B, 0, 1, True, False)
                values(B - 1, NSLOT - 1, 1)

                for n in range(NB):
                    pe.wait_ge(s_attn, B)
                    if n >= 2:
                        pe.wait_ge(s_proj_bias, n - 1)
                    for k in range(TPB):
                        last = pe.matmul(bank[n % 2][:, C * k:C * k + C], attn_T[:, BLK * n + P * k:BLK * n + P * k + P],
                                         w_T[:, 3, :], start=True, stop=True)
                    last.then_inc(s_proj_out, 1)

            @block.vector
            def _(v):
                v.wait_ge(s_masks, 1)
                nc.vector.tensor_reduce(head_in_group[:], head_of[:].rearrange("p (g h) -> p h g", g=G), AX.X,
                                        ALU.add).then_inc(s_masks_dve, 1)
                nc.vector.tensor_reduce(query_of[:], ident[:].rearrange("p (q n) -> p n q", n=N), AX.X, ALU.add)
                nc.vector.tensor_scalar(head_scaled[:], head_of[:], float(D) ** -0.5, None,
                                        ALU.mult).then_inc(s_masks_dve, 1)
                v.wait_ge(s_masks, 2)
                nc.vector.tensor_scalar(same_head_mean[:], same_head[:], 1.0 / D, None, ALU.mult).then_inc(s_masks_dve, 1)
                ln_vector(v, 0, lambda n: v.wait_ge(s_x_in[n], 16))

                def probs_out(b, par, h):
                    v.wait_ge(s_pT, 2 * b + (h + 1))
                    if not first(b, 2) and h == 0:
                        v.wait_ge(s_pv, b - 1)
                    nc.vector.tensor_copy(pT[:, par, h, :], bank[PT_BANK[h]][:]).then_inc(s_pT_out, 1)

                def normalise(b):
                    v.wait_ge(s_pv, b + 1)
                    nc.vector.tensor_tensor(o_masked[:], O_BANK[:, 0:P].rearrange("p (h n) -> p h n", h=HG),
                                            head_in_group[:].unsqueeze(2).broadcast_to([P, HG, N]),
                                            ALU.mult).then_inc(s_o_masked, 1)
                    v.wait_ge(s_o_masked, b + 1)
                    nc.vector.tensor_reduce(o_sum[:], o_masked[:].rearrange("p h n -> p n h"), AX.X, ALU.add).then_inc(s_o_sum, 1)
                    v.wait_ge(s_o_sum, b + 1)
                    nc.vector.tensor_tensor(attn_T[:, queries_of(b)], o_sum[:], O_BANK[:, P:P + N], ALU.mult).then_inc(s_attn, 1)

                def step(b, u):
                    par, before = u % 2, (u + 1) % 2
                    if not first(b, 2):
                        normalise(b - 2)
                    for h in range(2):
                        v.wait_ge(s_scores, 2 * b + (h + 1))
                        if h == 0 and not first(b, 2):
                            v.wait_ge(s_exp, 2 * b - 2)
                        nc.vector.tensor_reduce(
                            neg_max[:, par, 2 * h:2 * h + 2], psum[:, 2 * h:2 * h + 2, 0:KEYS], AX.X, ALU.max, negate=True).then_inc(s_max, 1)
                        if h == 0:
                            if not first(b, 1):
                                inverse(b - 1, before)
                                probs_out(b - 1, before, 1)
                        else:
                            probs_out(b, par, 0)

                def inverse(b, par):
                    v.wait_ge(s_exp, 2 * b + 2)
                    if not first(b, 2):
                        v.wait_ge(s_spread, b - 1)
                    nc.vector.reciprocal(inv_sum[:, par], row_sum[:, par]).then_inc(s_inv, 1)

                over_sequences(v, step)
                normalise(B - 2)
                probs_out(B - 1, 1, 1)
                inverse(B - 1, 1)
                normalise(B - 1)
                for n in range(NB):
                    v.wait_ge(s_proj_out, n + 1)
                    tiles = slice(TPB * n, TPB * n + TPB)
                    nc.vector.tensor_tensor(x_sq[:, tiles, :], bank[n % 2][:].rearrange("p (t c) -> p t c", c=C),
                                            b_rows[:].unsqueeze(1).broadcast_to([P, TPB, C]), ALU.add).then_inc(s_proj_bias, 1)
                    v.wait_ge(s_proj_bias, n + 1)
                    nc.vector.tensor_tensor(x_res[:, tiles, :], x_res[:, tiles, :], x_sq[:, tiles, :], ALU.add).then_inc(s_x1, 1)


        w_split = {(name, part): whole.enter_context(nc.sbuf_tensor(f"{name}_{part}", shape, F32R))
                   for name, shape in (("gate", [P, E, I]), ("up", [P, E, I]), ("shared_gate", [P, IS]), ("shared_up", [P, IS]))
                   for part in ("high", "low")}
        s_w_high = sem("s_w_high")
        s_w_low = sem("s_w_low")

        def weight_parts(name, e):
            routed, shared = {"gate": (w_gate, ws_gate), "up": (w_up, ws_up)}[name]
            if e < E:
                return routed[:, e, :], w_split[name, "high"][:, e, :], w_split[name, "low"][:, e, :]
            return shared[:], w_split["shared_" + name, "high"][:], w_split["shared_" + name, "low"][:]

        splits = [(name, e) for e in range(E + 1) for name in ("gate", "up")]

        with ExitStack() as scope:
            def tile(name, shape):
                return sb(name, shape, scope)

            LAG = 2
            params = tile("params", [P, NPAR])
            gn_eps = tile("gn_eps", [P, 1])
            v_weight = tile("v_weight", [P, D, C])
            to_column = tile("to_column", [P, D, C])
            diff = tile("diff", [P, 2, BLK])
            mixed_x = tile("mixed_x", [P, BLK])
            mix_hidden = tile("mix_hidden", [P, BLK])
            mix_hidden_last = tile("mix_hidden_last", [TM, BLK])
            mix_part = tile("mix_part", [P, 2, BLK])
            mixed = tile("mixed", [P, 2, 5, BLK])
            decay_hidden = tile("decay_hidden", [TD, BLK])
            decay = tile("decay", [P, 2, BLK])
            recep = tile("recep", [P, 2, BLK])
            key = tile("key", [P, 2, BLK])
            value = tile("value", [P, BLK])
            gate = tile("gate", [P, 2, BLK])
            bonus_in = tile("bonus_in", [P, BLK])
            bonus = tile("bonus", [P, 2, BLK])
            kv = tile("kv", [P, 2, BLK])
            state = tile("state", [P, LAG + 1, BLK])
            read = tile("read", [P, LAG + 1, BLK])
            y_sum, y_cen, y_sq, y_std = [x_sq[:, TPB * k:TPB * k + TPB, :].rearrange("p t c -> p (t c)") for k in range(4)]
            y_norm, y_affine, y_gated, decay_exp = [x_cen[:, TPB * k:TPB * k + TPB, :].rearrange("p t c -> p (t c)")
                                                    for k in range(4)]
            y_rstd = y_std

            names = """s_params_turned s_params s_vweight s_tocolumn s_diff s_mixed_x s_hidden s_hidden_out
                s_mix s_mix_out s_mixed s_dproj s_dhidden s_dproj2 s_dexp s_decay s_decay_cut
                s_recep s_key s_value s_gate s_bonus_in s_bonus s_kv s_state s_read s_y s_y_sum
                s_mean s_y_cen s_y_sq s_var s_y_std s_y_rstd s_y_norm s_y_affine s_y_gated s_out
                s_x2 s_used s_read_zero""".split()
            (s_params_turned, s_params, s_vweight, s_tocolumn, s_diff, s_mixed_x, s_hidden, s_hidden_out,
             s_mix, s_mix_out, s_mixed, s_dproj, s_dhidden, s_dproj2, s_dexp, s_decay, s_decay_cut,
             s_recep, s_key, s_value, s_gate, s_bonus_in, s_bonus, s_kv, s_state, s_read, s_y, s_y_sum,
             s_mean, s_y_cen, s_y_sq, s_var, s_y_std, s_y_rstd, s_y_norm, s_y_affine, s_y_gated, s_out,
             s_x2, s_used, s_read_zero) = [sem(n) for n in names]
            s_prod = sem("s_prod")
            s_prod_free = [sem("s_prod_free0"), sem("s_prod_free1")]

            HIDDEN, HIDDEN_LAST, MIX = bank[0], bank[1], (2, 3)
            PROD, Y, POST = (4, 5), bank[6], bank[7]
            SEQ, WITHIN = "p (s n) -> p s n", N

            def mixing(n):
                return [("hidden", n)] + [("mix", n, f) for f in range(5)]

            order = [("shift", 0)] + mixing(0)
            for n in range(NB):
                order.append(("project", n, "decay1"))
                if n:
                    order.append(("y", n - 1, D - 2))
                order.append(("project", n, "r"))
                if n:
                    order += [("y", n - 1, D - 1), ("sum", n - 1)]
                order += [("project", n, k) for k in ("k", "v", "decay2", "g")]
                order.append(("bonus_in", n))
                for j in range(D):
                    order.append(("state", n, j))
                    if j == 1 and n + 1 < NB:
                        order.append(("shift", n + 1))
                    if j >= LAG:
                        order.append(("y", n, j - LAG))
                    if n:
                        order += [(name, n - 1) for name, when in (("mean", 0), ("variance", 1), ("inverse0", 2), ("inverse1", 3),
                                                            ("norm", 4), ("gated", 5), ("output", 7))
                                  if j == when]
                    if j == 1:
                        order.append(("bonus", n))
                    if j >= 2 and n + 1 < NB:
                        order.append(mixing(n + 1)[j - 2])
            order += [("y", NB - 1, D - 2), ("y", NB - 1, D - 1)]
            order += [(name, NB - 1) for name in ("sum", "mean", "variance", "inverse0", "inverse1", "norm", "gated", "output")]
            prod_no = {}
            for s in order:
                if s[0] == "project":
                    prod_no[(s[2], s[1])] = len(prod_no)
                elif s[0] in ("state", "bonus"):
                    prod_no[s] = len(prod_no)

            def prod_bank(key_):
                return bank[PROD[prod_no[key_] % 2]]

            block = scope.enter_context(nc.Block())

            @block.gpsimd
            def _(pool):
                g = nc.gpsimd
                ln_gpsimd(pool, 1)
                g.memset(read[:], 0.0)
                g.memset(gn_eps[:], GN_EPS)
                g.memset(to_column[:], 0.0).then_inc(s_read_zero, 1)
                pool.wait_ge(s_time_w_in, 16 * TIME_W_DMAS)
                for j in range(D):
                    last = g.tensor_copy(v_weight[:, j, :].rearrange("p (h i) -> p h i", h=H),
                                         w_time[:, W_V, :].rearrange("p (h j) -> p h j", h=H)[:, :, j:j + 1].broadcast_to([P, H, D]))
                last.then_inc(s_vweight, 1)
                pool.wait_ge(s_read_zero, 1)
                for j in range(D):
                    last = g.tensor_copy(to_column[:, j, :].rearrange("p (h j) -> p h j", h=H)[:, :, j], head_of[:])
                last.then_inc(s_tocolumn, 1)
                for s in order:
                    n = s[1]
                    par = n % 2
                    if s[0] == "mix":
                        f = s[2]
                        pool.wait_ge(s_mix_out, 5 * n + f + 1)
                        if n >= 2:
                            pool.wait_ge(s_prod, prod_no[("state", n - 2, D - 1)] + 1)
                        g.tensor_tensor(mixed[:, par, f, :], mix_part[:, (5 * n + f) % 2, :],
                                        ln_T[:, BLK * n:BLK * n + BLK], ALU.add).then_inc(s_mixed, 1)
                    elif s == ("project", n, "decay2"):
                        pool.wait_ge(s_decay, n + 1)
                        g.memset(decay[:, par].rearrange(SEQ, n=N)[:, :, 0:1], 0.0).then_inc(s_decay_cut, 1)
                    elif s[0] == "state":
                        q = D * n + s[2]
                        pool.wait_ge(s_state, q + 1)
                        pool.wait_ge(s_recep, n + 1)
                        if q > LAG:
                            pool.wait_ge(s_y, q - LAG)
                        g.tensor_tensor(read[:, q % (LAG + 1)].rearrange(SEQ, n=N)[:, :, 1:N],
                                        recep[:, par].rearrange(SEQ, n=N)[:, :, 1:N],
                                        state[:, q % (LAG + 1)].rearrange(SEQ, n=N)[:, :, 0:N - 1], ALU.mult).then_inc(s_read, 1)
                        if 1 <= q <= len(splits):
                            pool.wait_ge(s_w_high, q)
                            exact, high, low = weight_parts(*splits[q - 1])
                            g.tensor_tensor(low, exact, high.bitcast(F32), ALU.subtract).then_inc(s_w_low, 1)
                    elif s[0] == "gated":
                        pool.wait_ge(s_y_affine, n + 1)
                        pool.wait_ge(s_gate, n + 1)
                        if n:
                            pool.wait_ge(s_out, n)
                        g.tensor_tensor(y_gated[:], y_affine[:], gate[:, par], ALU.mult).then_inc(s_y_gated, 1)

            @block.scalar
            def _(act):
                ln_scalar_square(act, 1, range(NB - 1))
                ln_scalar_evacuate(act, 1, (0, 1), [0])
                ln_scalar_square(act, 1, [NB - 1])
                ln_scalar_evacuate(act, 1, (0, 1), range(1, NB))
                act.wait_ge(s_params_turned, 1)
                nc.scalar.copy(params[:], bank[2][:, 0:NPAR]).then_inc(s_params, 1)

                for s in order:
                    n = s[1]
                    par = n % 2
                    if s[0] == "hidden":
                        act.wait_ge(s_hidden, n + 1)
                        if n:
                            act.wait_ge(s_mix, 5 * n)
                        nc.scalar.activation(mix_hidden[:], HIDDEN[:], ACT.Tanh)
                        nc.scalar.activation(mix_hidden_last[:], HIDDEN_LAST[0:TM, :], ACT.Tanh).then_inc(s_hidden_out, 1)
                    elif s[0] == "project":
                        act.wait_ge(s_prod, prod_no[(s[2], n)] + 1)
                        source = prod_bank((s[2], n))
                        if s[2] == "decay1":
                            act.wait_ge(s_params, 1)
                            nc.scalar.activation(decay_hidden[:], source[0:TD, :], ACT.Tanh).then_inc(s_dhidden, 1)
                        elif s[2] == "r":
                            if n >= 2:
                                act.wait_ge(s_read, D * (n - 1))
                            nc.scalar.copy(recep[:, par], source).then_inc(s_recep, 1)
                        elif s[2] == "k":
                            if n >= 2:
                                act.wait_ge(s_kv, D * (n - 1))
                            nc.scalar.copy(key[:, par], source).then_inc(s_key, 1)
                        elif s[2] == "v":
                            if n:
                                act.wait_ge(s_bonus, n)
                            nc.scalar.copy(value[:], source).then_inc(s_value, 1)
                        elif s[2] == "decay2":
                            nc.scalar.activation(decay_exp[:], source, ACT.Exp,
                                                 bias=params[:, PAR_DECAY:PAR_DECAY + 1]).then_inc(s_dexp, 1)
                            act.wait_ge(s_dexp, n + 1)
                            if n >= 2:
                                act.wait_ge(s_state, D * (n - 1))
                            nc.scalar.activation(decay[:, par], decay_exp[:], ACT.Exp, scale=-1.0).then_inc(s_decay, 1)
                        else:
                            if n >= 2:
                                act.wait_ge(s_y_gated, n - 1)
                            nc.scalar.activation(gate[:, par], source, ACT.Silu).then_inc(s_gate, 1)
                    elif s[0] == "state" and D * n + s[2] < len(splits):
                        act.wait_ge(s_ffn_w_in, 16 * FFN_W_DMAS)
                        exact, high, low = weight_parts(*splits[D * n + s[2]])
                        nc.scalar.copy(high, exact).then_inc(s_w_high, 1)
                    elif s[0] == "mean":
                        act.wait_ge(s_y_cen, n + 1)
                        if n:
                            act.wait_ge(s_var, n)
                        nc.scalar.activation(y_sq[:], y_cen[:], ACT.Square).then_inc(s_y_sq, 1)
                    elif s[0] == "variance":
                        act.wait_ge(s_var, n + 1)
                        act.wait_ge(s_read_zero, 1)
                        if n:
                            act.wait_ge(s_y_norm, n)
                        nc.scalar.activation(y_std[:], POST, ACT.Sqrt, bias=gn_eps[:]).then_inc(s_y_std, 1)
                    elif s[0] == "norm":
                        act.wait_ge(s_y_norm, n + 1)
                        if n:
                            act.wait_ge(s_y_gated, n)
                        nc.scalar.activation(y_affine[:], y_norm[:], ACT.Identity, scale=params[:, PAR_LN_W:PAR_LN_W + 1],
                                             bias=params[:, PAR_LN_B:PAR_LN_B + 1]).then_inc(s_y_affine, 1)

            @block.tensor
            def _(pe):
                pe.wait_ge(s_time_w_in, 16 * TIME_W_DMAS)
                pe.transpose(bank[2][:, 0:NPAR], param_rows[:], ident[0:NPAR, 0:NPAR]).then_inc(s_params_turned, 1)
                ln_tensor(pe, 1, (0, 1))

                def freed_by(key_):
                    n = key_[1]
                    return {"decay1": (s_dhidden, n + 1), "decay2": (s_dexp, n + 1), "r": (s_recep, n + 1),
                            "k": (s_key, n + 1), "v": (s_value, n + 1), "g": (s_gate, n + 1),
                            "bonus": (s_bonus, n + 1), "state": (s_kv, D * n + key_[-1] + 1)}[key_[0]]

                by_no = {no: key_ for key_, no in prod_no.items()}

                def product(key_, lhsT, rhs, rows=P):
                    no = prod_no[key_]
                    if no >= 2:
                        pe.wait_ge(*freed_by(by_no[no - 2]))
                    pe.matmul(prod_bank(key_)[0:rows, :], lhsT, rhs, start=True, stop=True).then_inc(s_prod, 1)

                for s in order:
                    n = s[1]
                    par = n % 2
                    if s[0] == "hidden":
                        pe.wait_ge(s_mixed_x, n + 1)
                        if n == 0:
                            pe.wait_ge(s_ln_T, 2 * NB)
                            pe.wait_ge(s_params, 1)
                        else:
                            pe.wait_ge(s_hidden_out, n)
                        pe.matmul(HIDDEN, mix_w1[:, 0:4 * TM], mixed_x[:], start=True, stop=True)
                        pe.matmul(HIDDEN_LAST[0:TM, :], mix_w1[:, 4 * TM:5 * TM], mixed_x[:], start=True, stop=True).then_inc(s_hidden, 1)
                    elif s[0] == "mix":
                        f = s[2]
                        m = 5 * n + f
                        pe.wait_ge(s_hidden_out, n + 1)
                        if m >= 2:
                            pe.wait_ge(s_mix_out, m - 1)
                        rows = slice(TM * f, TM * f + TM)
                        w2, hid = (mix_w2[rows, :], mix_hidden[rows, :]) if f < 4 else (mix_w2_last[:], mix_hidden_last[:])
                        pe.matmul(bank[MIX[m % 2]], w2, hid, start=True, stop=True).then_inc(s_mix, 1)
                    elif s[0] == "project":
                        if s[2] == "decay1":
                            pe.wait_ge(s_mixed, 5 * n + 1)
                            product(("decay1", n), decay_w1[:], mixed[:, par, 0, :], TD)
                        elif s[2] == "decay2":
                            pe.wait_ge(s_dhidden, n + 1)
                            product(("decay2", n), decay_w2[:], decay_hidden[:])
                        else:
                            w, f = {"r": (W_R, 3), "k": (W_K, 1), "v": (W_V, 2), "g": (W_G, 4)}[s[2]]
                            pe.wait_ge(s_mixed, 5 * n + f + 1)
                            product((s[2], n), w_time[:, w, :], mixed[:, par, f, :])
                    elif s[0] == "bonus":
                        pe.wait_ge(s_bonus_in, n + 1)
                        product(s, same_head[:], bonus_in[:])
                    elif s[0] == "state":
                        pe.wait_ge(s_vweight, 1)
                        product(s, v_weight[:, s[2], :], mixed[:, par, 2, :])
                    elif s[0] == "y":
                        j = s[2]
                        q = D * n + j
                        pe.wait_ge(s_tocolumn, 1)
                        pe.wait_ge(s_read, q + 1)
                        if j == 0 and n:
                            pe.wait_ge(s_y_sum, n)
                        pe.matmul(Y, to_column[:, j, :], read[:, q % (LAG + 1)], start=(j == 0), stop=(j == D - 1)).then_inc(s_y, 1)
                    elif s[0] == "mean":
                        pe.wait_ge(s_y_sum, n + 1)
                        if n:
                            pe.wait_ge(s_x2, n)
                        pe.matmul(POST, same_head_mean[:], y_sum[:], start=True, stop=True).then_inc(s_mean, 1)
                    elif s[0] == "variance":
                        pe.wait_ge(s_y_sq, n + 1)
                        pe.wait_ge(s_y_cen, n + 1)
                        pe.matmul(POST, same_head_mean[:], y_sq[:], start=True, stop=True).then_inc(s_var, 1)
                    elif s[0] == "output":
                        pe.wait_ge(s_y_std, n + 1)
                        pe.wait_ge(s_y_gated, n + 1)
                        for k in range(TPB):
                            last = pe.matmul(POST[:, C * k:C * k + C], y_gated[:, P * k:P * k + P], w_time[:, W_O, :],
                                             start=True, stop=True)
                        last.then_inc(s_out, 1)

            @block.vector
            def _(v):
                ln_vector(v, 1)
                v.wait_ge(s_params, 1)
                for s in order:
                    n = s[1]
                    par = n % 2
                    cols = slice(BLK * n, BLK * n + BLK)
                    if s[0] == "shift":
                        v.wait_ge(s_ln_T, NB + n + 1)
                        x = ln_T[:, cols].rearrange(SEQ, n=N)
                        dx = diff[:, par].rearrange(SEQ, n=N)
                        if n >= 2:
                            v.wait_ge(s_mix_out, 5 * (n - 1))
                        nc.vector.tensor_tensor(dx[:, :, 1:N], x[:, :, 0:N - 1], x[:, :, 1:N], ALU.subtract)
                        nc.vector.tensor_scalar(dx[:, :, 0:1], x[:, :, 0:1], -1.0, None, ALU.mult).then_inc(s_diff, 1)
                        v.wait_ge(s_diff, n + 1)
                        if n:
                            v.wait_ge(s_hidden, n)
                        nc.vector.scalar_tensor_tensor(mixed_x[:], diff[:, par], params[:, PAR_X:PAR_X + 1],
                                                       ln_T[:, cols], ALU.mult, ALU.add).then_inc(s_mixed_x, 1)
                    elif s[0] == "mix":
                        f = s[2]
                        k = (PAR_W, PAR_K, PAR_V, PAR_R, PAR_G)[f]
                        m = 5 * n + f
                        v.wait_ge(s_mix, m + 1)
                        if m >= 2:
                            v.wait_ge(s_mixed, m - 1)
                        nc.vector.scalar_tensor_tensor(mix_part[:, m % 2, :], bank[MIX[m % 2]], params[:, k:k + 1],
                                                       diff[:, par], ALU.add, ALU.mult).then_inc(s_mix_out, 1)
                    elif s[0] == "bonus_in":
                        v.wait_ge(s_recep, n + 1)
                        v.wait_ge(s_key, n + 1)
                        if n:
                            v.wait_ge(s_bonus, n)
                        nc.vector.scalar_tensor_tensor(bonus_in[:], recep[:, par], params[:, PAR_BONUS:PAR_BONUS + 1],
                                                       key[:, par], ALU.mult, ALU.mult).then_inc(s_bonus_in, 1)
                    elif s[0] == "bonus":
                        v.wait_ge(s_prod, prod_no[("bonus", n)] + 1)
                        v.wait_ge(s_value, n + 1)
                        if n >= 2:
                            v.wait_ge(s_y_sum, n - 1)
                        nc.vector.tensor_tensor(bonus[:, par], prod_bank(("bonus", n)), value[:], ALU.mult).then_inc(s_bonus, 1)
                    elif s[0] == "state":
                        q = D * n + s[2]
                        v.wait_ge(s_prod, prod_no[s] + 1)
                        v.wait_ge(s_key, n + 1)
                        if q >= 2:
                            v.wait_ge(s_state, q - 1)
                        nc.vector.tensor_tensor(kv[:, q % 2], prod_bank(s), key[:, par], ALU.mult).then_inc(s_kv, 1)
                        v.wait_ge(s_kv, q + 1)
                        v.wait_ge(s_decay_cut, n + 1)
                        if q > LAG:
                            v.wait_ge(s_read, q - LAG)
                        nc.vector.tensor_tensor_scan(state[:, q % (LAG + 1)], decay[:, par], kv[:, q % 2], 0.0,
                                                     ALU.mult, ALU.add).then_inc(s_state, 1)
                    elif s[0] == "sum":
                        v.wait_ge(s_y, D * n + D)
                        v.wait_ge(s_bonus, n + 1)
                        if n:
                            v.wait_ge(s_y_cen, n)
                            v.wait_ge(s_mean, n)
                        nc.vector.tensor_tensor(y_sum[:], Y, bonus[:, par], ALU.add).then_inc(s_y_sum, 1)
                    elif s[0] == "mean":
                        v.wait_ge(s_mean, n + 1)
                        v.wait_ge(s_y_sum, n + 1)
                        if n:
                            v.wait_ge(s_y_norm, n)
                            v.wait_ge(s_y_sq, n)
                        nc.vector.tensor_tensor(y_cen[:], y_sum[:], POST, ALU.subtract).then_inc(s_y_cen, 1)
                    elif s[0] in ("inverse0", "inverse1"):
                        half = int(s[0][-1])
                        part = slice(BLK // 2 * half, BLK // 2 * (half + 1))
                        v.wait_ge(s_y_std, n + 1)
                        if n:
                            v.wait_ge(s_y_norm, n)
                        nc.vector.reciprocal(y_rstd[:, part], y_std[:, part]).then_inc(s_y_rstd, 1)
                    elif s[0] == "norm":
                        v.wait_ge(s_y_rstd, 2 * n + 2)
                        if n:
                            v.wait_ge(s_y_affine, n)
                        nc.vector.tensor_tensor(y_norm[:], y_cen[:], y_rstd[:], ALU.mult).then_inc(s_y_norm, 1)
                    elif s[0] == "output":
                        v.wait_ge(s_out, n + 1)
                        tiles = slice(TPB * n, TPB * n + TPB)
                        nc.vector.tensor_tensor(x_res[:, tiles, :], x_res[:, tiles, :],
                                                POST.rearrange("p (t c) -> p t c", c=C), ALU.add).then_inc(s_x2, 1)


        with ExitStack() as scope:
            def tile(name, shape):
                return sb(name, shape, scope)

            logits = tile("logits", [P, NT, E])
            rank = tile("rank", [P, E])
            best = tile("best", [P, NT])
            is_best = tile("is_best", [P, NT, E])
            best_rank = tile("best_rank", [P, NT])
            first_hot = tile("first_hot", [P, NT, E])
            others = tile("others", [P, NT, E])
            second = tile("second", [P, NT])
            is_second = tile("is_second", [P, NT, E])
            second_rank = tile("second_rank", [P, NT])
            second_hot = tile("second_hot", [P, NT, E])
            gap = tile("gap", [P, NT])
            gap_exp = tile("gap_exp", [P, NT])
            gap_den = tile("gap_den", [P, NT])
            prob_first = tile("prob_first", [P, NT])
            prob_second = tile("prob_second", [P, NT])
            share_first = tile("share_first", [P, NT, E])
            share_second = tile("share_second", [P, NT, E])
            combine = tile("combine", [P, NT, E])
            silu = tile("silu", [P, 2, BLK])
            hidden = tile("hidden", [P, 2, len(expert_chunks(I)), BLK])

            x_high = scope.enter_context(nc.sbuf_tensor("x_high", [P, B * N], F32R))
            x_low = scope.enter_context(nc.sbuf_tensor("x_low", [P, B * N], F32R))

            s_x_high = sem("s_x_high")
            s_x_low = sem("s_x_low")
            s_logits = sem("s_logits")
            s_logits_out = sem("s_logits_out")
            s_rank = sem("s_rank")
            s_top = sem("s_top")
            s_gap_exp = sem("s_gap_exp")
            s_up = sem("s_up")
            s_silu = sem("s_silu")
            s_hidden_done = sem("s_hidden_done")
            s_down = sem("s_down")
            s_acc = sem("s_acc")
            s_stored = sem("s_stored")

            GATE_BANK, UP_BANK, DOWN_BANK = (0, 1), (2, 3), (4, 5)
            experts = [(e, expert_chunks(I)) for e in range(E)] + [(E, expert_chunks(IS))]
            NEX = len(experts)
            pieces = [(e, k, start, size) for e, chunks in experts for k, (start, size) in enumerate(chunks)]
            NPIECE = len(pieces)
            assert NPIECE % 2 == 0
            last_piece = {e: q for q, (e, _, _, _) in enumerate(pieces)}

            TOP_GAP = 9

            def over_blocks(eng, body):
                body(0)
                with eng.Fori(1, NB) as n:
                    body(n)

            def later(n, q):
                return q >= 2 or not isinstance(n, int)

            block = scope.enter_context(nc.Block())

            @block.sync
            def _(sp):
                for n in range(NB):
                    sp.wait_ge(s_acc, NEX * (n + 1))
                    tiles = slice(TPB * n, TPB * n + TPB)
                    sp.dma_start(out_tiles[:, tiles, :], x_res[:, tiles, :]).then_inc(s_stored, 16)
                sp.wait_ge(s_stored, 16 * NB)

            @block.gpsimd
            def _(pool):
                for e in range(E):
                    last = nc.gpsimd.memset(rank[:, e:e + 1], float(E - e))
                last.then_inc(s_rank, 1)
                ln_gpsimd(pool, 2)
                for n in range(NB):
                    cols = slice(BLK * n, BLK * n + BLK)
                    pool.wait_ge(s_ln_T, 2 * NB + n + 1)
                    pool.wait_ge(s_x_high, n + 1)
                    nc.gpsimd.tensor_tensor(x_low[:, cols], ln_T[:, cols], x_high[:, cols].bitcast(F32),
                                            ALU.subtract).then_inc(s_x_low, 1)

            @block.scalar
            def _(act):
                ln_scalar_square(act, 2, range(NB - 1))
                for n in range(NB):
                    if n == 1:
                        ln_scalar_square(act, 2, [NB - 1])
                    cols = slice(BLK * n, BLK * n + BLK)
                    act.wait_ge(s_ln_turned, NB * 2 + n + 1)
                    nc.scalar.copy(x_high[:, cols], bank[(6, 7)[n % 2]][:]).then_inc(s_x_high, 1)
                    nc.scalar.copy(ln_T[:, cols], bank[(6, 7)[n % 2]][:]).then_inc(s_ln_T, 1)
                act.wait_ge(s_logits, 1)
                nc.scalar.copy(logits[:].rearrange("p t e -> p (t e)"), bank[6][:, 0:NT * E]).then_inc(s_logits_out, 1)
                act.wait_ge(s_top, TOP_GAP)
                nc.scalar.activation(gap_exp[:], gap[:], ACT.Exp).then_inc(s_gap_exp, 1)

                def body(n):
                    for q, (e, k, start, size) in enumerate(pieces):
                        act.wait_ge(s_up, NPIECE * n + (q + 1))
                        if later(n, q):
                            act.wait_ge(s_hidden_done, NPIECE * n + (q - 1))
                        nc.scalar.activation(silu[0:size, q % 2, :], bank[GATE_BANK[q % 2]][0:size], ACT.Silu).then_inc(s_silu, 1)

                over_blocks(act, body)

            @block.tensor
            def _(pe):
                ln_tensor(pe, 2, (6, 7))
                pe.wait_ge(s_ln_T, 3 * NB)
                for k in range(NT):
                    last = pe.matmul(bank[6][:, E * k:E * k + E], ln_T[:, P * k:P * k + P], gate_w[:], start=True, stop=True)
                last.then_inc(s_logits, 1)
                pe.wait_ge(s_ffn_w_in, 16 * FFN_W_DMAS)
                pe.wait_ge(s_x_high, NB)
                pe.wait_ge(s_x_low, NB)
                pe.wait_ge(s_w_high, len(splits))
                pe.wait_ge(s_w_low, len(splits))

                def split_product(out, name, e, start, size, n):
                    exact, high, low = weight_parts(name, e)
                    cols = bass.ds(n * BLK, BLK)
                    pe.matmul(out, high[:, start:start + size], x_high[:, cols], start=True, stop=False)
                    pe.matmul(out, high[:, start:start + size], x_low[:, cols], start=False, stop=False)
                    return pe.matmul(out, low[:, start:start + size], x_high[:, cols], start=False, stop=True)

                def down(n, e, chunks):
                    pe.wait_ge(s_hidden_done, NPIECE * n + (last_piece[e] + 1))
                    if later(n, e):
                        pe.wait_ge(s_acc, NEX * n + (e - 1))
                    for k in range(TPB):
                        for c, (start, size) in enumerate(chunks):
                            w = w_down[0:size, e, c, :] if e < E else ws_down[0:size, c, :]
                            last = pe.matmul(bank[DOWN_BANK[e % 2]][:, C * k:C * k + C],
                                             hidden[0:size, e % 2, c, P * k:P * k + P], w,
                                             start=(c == 0), stop=(c == len(chunks) - 1))
                    last.then_inc(s_down, 1)

                def body(n):
                    for e, chunks in experts:
                        for q, (e_, k, start, size) in enumerate(pieces):
                            if e_ != e:
                                continue
                            if later(n, q):
                                pe.wait_ge(s_hidden_done, NPIECE * n + (q - 1))
                            split_product(bank[GATE_BANK[q % 2]][0:size], "gate", e, start, size, n)
                            split_product(bank[UP_BANK[q % 2]][0:size], "up", e, start, size, n).then_inc(s_up, 1)
                        if e:
                            down(n, *experts[e - 1])
                    down(n, *experts[-1])

                over_blocks(pe, body)

            @block.vector
            def _(v):
                ln_vector(v, 2)
                done = [0]

                def step(ins):
                    done[0] += 1
                    ins.then_inc(s_top, 1)
                    v.wait_ge(s_top, done[0])

                def over_experts(a):
                    return a[:].unsqueeze(2).broadcast_to([P, NT, E])

                ranks = rank[:].unsqueeze(1).broadcast_to([P, NT, E])
                v.wait_ge(s_logits_out, 1)
                v.wait_ge(s_rank, 1)
                step(nc.vector.tensor_reduce(best[:], logits[:], AX.X, ALU.max))
                step(nc.vector.tensor_tensor(is_best[:], logits[:], over_experts(best), ALU.is_equal))
                step(nc.vector.tensor_tensor(is_best[:], is_best[:], ranks, ALU.mult))
                step(nc.vector.tensor_reduce(best_rank[:], is_best[:], AX.X, ALU.max))
                step(nc.vector.tensor_tensor(first_hot[:], is_best[:], over_experts(best_rank), ALU.is_equal))
                step(nc.vector.scalar_tensor_tensor(others[:], first_hot[:], -3e38, logits[:], ALU.mult, ALU.add))
                step(nc.vector.tensor_reduce(second[:], others[:], AX.X, ALU.max))
                step(nc.vector.tensor_tensor(is_second[:], others[:], over_experts(second), ALU.is_equal))
                step(nc.vector.tensor_tensor(gap[:], second[:], best[:], ALU.subtract))
                step(nc.vector.tensor_tensor(is_second[:], is_second[:], ranks, ALU.mult))
                step(nc.vector.tensor_reduce(second_rank[:], is_second[:], AX.X, ALU.max))
                step(nc.vector.tensor_tensor(second_hot[:], is_second[:], over_experts(second_rank), ALU.is_equal))
                v.wait_ge(s_gap_exp, 1)
                step(nc.vector.tensor_scalar(gap_den[:], gap_exp[:], 1.0, None, ALU.add))
                step(nc.vector.reciprocal(prob_first[:], gap_den[:]))
                step(nc.vector.tensor_tensor(prob_second[:], gap_exp[:], prob_first[:], ALU.mult))
                step(nc.vector.tensor_tensor(share_first[:], first_hot[:], over_experts(prob_first), ALU.mult))
                step(nc.vector.tensor_tensor(share_second[:], second_hot[:], over_experts(prob_second), ALU.mult))
                step(nc.vector.tensor_tensor(combine[:], share_first[:], share_second[:], ALU.add))

                def accumulate(n, e):
                    v.wait_ge(s_down, NEX * n + (e + 1))
                    if not (isinstance(n, int) and e == 0):
                        v.wait_ge(s_acc, NEX * n + e)
                    out_bank = bank[DOWN_BANK[e % 2]]
                    if e < E:
                        for k in range(TPB):
                            row = x_res[:, bass.ds(n * TPB + k, 1), :].rearrange("p a c -> p (a c)")
                            share = combine[:, bass.ds(n * TPB + k, 1), e:e + 1].rearrange("p a e -> p (a e)")
                            last = nc.vector.scalar_tensor_tensor(row, out_bank[:, C * k:C * k + C], share, row, ALU.mult, ALU.add)
                    else:
                        rows = x_res[:, bass.ds(n * TPB, TPB), :]
                        last = nc.vector.tensor_tensor(rows, out_bank.rearrange("p (t c) -> p t c", c=C), rows, ALU.add)
                    last.then_inc(s_acc, 1)

                def body(n):
                    for e, chunks in experts:
                        for q, (e_, k, start, size) in enumerate(pieces):
                            if e_ != e:
                                continue
                            v.wait_ge(s_silu, NPIECE * n + (q + 1))
                            if k == 0 and later(n, e):
                                v.wait_ge(s_down, NEX * n + (e - 1))
                            nc.vector.tensor_tensor(hidden[0:size, e % 2, k, :], silu[0:size, q % 2, :],
                                                    bank[UP_BANK[q % 2]][0:size], ALU.mult).then_inc(s_hidden_done, 1)
                        if e:
                            accumulate(n, e - 1)
                    accumulate(n, E)

                over_blocks(v, body)


_INS = ['x', 'ctx_2048', 'L0_xattn_w_qkv', 'L0_xattn_w_proj', 'L0_xattn_b_proj',
        'L0_attn_time_maa_x', 'L0_attn_time_maa_w', 'L0_attn_time_maa_k', 'L0_attn_time_maa_v',
        'L0_attn_time_maa_r', 'L0_attn_time_maa_g', 'L0_attn_time_maa_w1', 'L0_attn_time_maa_w2',
        'L0_attn_time_decay', 'L0_attn_time_decay_w1', 'L0_attn_time_decay_w2', 'L0_attn_time_faaaa',
        'L0_attn_W_r', 'L0_attn_W_k', 'L0_attn_W_v', 'L0_attn_W_g', 'L0_attn_W_o',
        'L0_attn_ln_w', 'L0_attn_ln_b', 'L0_ffn_gate_w', 'L0_ffn_Wg', 'L0_ffn_Wu', 'L0_ffn_Wd',
        'L0_ffn_Sg', 'L0_ffn_Su', 'L0_ffn_Sd']


def kernel(**inputs):
    import numpy as _np
    import concourse.bacc as _bacc
    from concourse import mybir as _mybir
    from concourse.bass_utils import run_bass_kernel_spmd as _run

    nc = _bacc.Bacc("TRN2", target_bir_lowering=False, num_devices=1)
    arrays, handles = {}, {}
    for name in _INS:
        a = _np.ascontiguousarray(inputs[name])
        arrays[f"in_{name}"] = a
        handles[name] = nc.dram_tensor(f"in_{name}", a.shape, _mybir.dt.from_np(a.dtype), kind="ExternalInput").ap()
    out = nc.dram_tensor("out_0", (B, N, C), F32, kind="ExternalOutput").ap()
    perceiver_layer(nc, handles, out)
    r = _run(nc, [arrays], core_ids=[0])
    return r.results[0]["out_0"]
```
